# Optimizing a Trainium2 kernel written in Bass

```python
import numpy as np
import jax
import jax.numpy as jnp

def _softmax(x, axis=-1):
    return jax.nn.softmax(x, axis=axis)

def _gelu(x):
    return jax.nn.gelu(x, approximate=True)

def _silu(x):
    return jax.nn.silu(x)

def _sigmoid(x):
    return jax.nn.sigmoid(x)

def _layernorm(x, axis=-1, eps=1e-05):
    m = jnp.mean(x, axis=axis, keepdims=True)
    v = jnp.var(x, axis=axis, keepdims=True)
    return (x - m) / jnp.sqrt(v + eps)

def _scatter_add(tgt, idx, src, axis=0):
    return tgt.at[idx].add(src)

def _segment_sum(src, seg, n):
    return jax.ops.segment_sum(src, seg, n)
kernel_name = 'mk_adj_seq_d2_adj_r2_ea9f03'

def setup_inputs(seed: int=0):
    np.random.seed(seed)
    _w = jnp.asarray

    def _rec_inputs():
        import jax
        import jax.numpy as jnp
        _gk = jax.random.key(seed)
        x = -0.0002928 + 1 * jax.random.normal(jax.random.fold_in(_gk, 1), (128, 128, 256), jnp.float32)
        _a = jax.random.bernoulli(jax.random.fold_in(_gk, 2), 0.0625, (128, 128, 128))
        _a = jnp.logical_or(_a, jnp.eye(128, dtype=bool))
        adj = _a.astype(jnp.int32)
        return (x, adj)
    x, adj = _rec_inputs()

    def _L0_gnn_setup():
        import jax, jax.numpy as jnp
        import numpy as np
        B, N, D, H = (4, 1024, 256, 8)
        HD = D // H
        EPS = 1e-05
        key = jax.random.key(seed)
        ks = jax.random.split(key, 12)
        x = jax.random.normal(ks[0], (B, N, D), dtype=jnp.float32)
        adj = jax.random.randint(ks[1], (B, N, N), 0, 2, dtype=jnp.int32)
        adj = jnp.maximum(adj, jnp.eye(N, dtype=jnp.int32)[None, :, :])
        s = 1.0 / np.sqrt(D)
        Wq = jax.random.uniform(ks[2], (D, D), jnp.float32, -s, s)
        bq = jnp.zeros((D,), jnp.float32)
        Wk = jax.random.uniform(ks[3], (D, D), jnp.float32, -s, s)
        bk = jnp.zeros((D,), jnp.float32)
        Wv = jax.random.uniform(ks[4], (D, D), jnp.float32, -s, s)
        bv = jnp.zeros((D,), jnp.float32)
        Wo = jax.random.uniform(ks[5], (D, D), jnp.float32, -s, s)
        bo = jnp.zeros((D,), jnp.float32)
        gamma = jnp.ones((D,), jnp.float32)
        beta = jnp.zeros((D,), jnp.float32)
        return {'x': x, 'adj': adj, 'Wq': Wq, 'bq': bq, 'Wk': Wk, 'bk': bk, 'Wv': Wv, 'bv': bv, 'Wo': Wo, 'bo': bo, 'gamma': gamma, 'beta': beta}
    _L0_gnn_all = _L0_gnn_setup()
    _L0_gnn_in = {k: v for k, v in _L0_gnn_all.items() if k in ('Wq', 'bq', 'Wk', 'bk', 'Wv', 'bv', 'Wo', 'bo', 'gamma', 'beta')}
    del _L0_gnn_all

    def _L1_gnn_setup():
        import jax, jax.numpy as jnp
        import numpy as np
        B, S, D, H = (2, 1024, 256, 8)
        HD = D // H
        EPS = 1e-05

        def _ln(x, g, b):
            mu = jnp.mean(x, axis=-1, keepdims=True)
            var = jnp.mean((x - mu) ** 2, axis=-1, keepdims=True)
            return (x - mu) * jax.lax.rsqrt(var + EPS) * g + b
        key = jax.random.key(seed)
        ks = jax.random.split(key, 16)
        x = jax.random.normal(ks[0], (B, S, D), dtype=jnp.float32)
        adj = jax.random.randint(ks[1], (B, S, S), 0, 2, dtype=jnp.int32)
        adj = adj.at[:, jnp.arange(S), jnp.arange(S)].set(1)
        edge_attr = jax.random.normal(ks[2], (B, S, S), dtype=jnp.float32)
        sc = 1.0 / np.sqrt(D)
        p = lambda k, shp: jax.random.normal(k, shp, dtype=jnp.float32) * sc
        return {'x': x, 'adj_matrix': adj, 'edge_attr_matrix': edge_attr, 'ln1_g': jnp.ones((D,)), 'ln1_b': jnp.zeros((D,)), 'ln2_g': jnp.ones((D,)), 'ln2_b': jnp.zeros((D,)), 'wq': p(ks[3], (D, D)), 'bq': jnp.zeros((D,)), 'wk': p(ks[4], (D, D)), 'bk': jnp.zeros((D,)), 'wv': p(ks[5], (D, D)), 'bv': jnp.zeros((D,)), 'wo': p(ks[6], (D, D)), 'bo': jnp.zeros((D,)), 'w1': p(ks[7], (D, 4 * D)), 'b1': jnp.zeros((4 * D,)), 'w2': p(ks[8], (4 * D, D)), 'b2': jnp.zeros((D,))}
    _L1_gnn_all = _L1_gnn_setup()
    _L1_gnn_in = {k: v for k, v in _L1_gnn_all.items() if k in ('ln1_g', 'ln1_b', 'ln2_g', 'ln2_b', 'wq', 'bq', 'wk', 'bk', 'wv', 'bv', 'wo', 'bo', 'w1', 'b1', 'w2', 'b2')}
    del _L1_gnn_all
    return {'x': x, 'adj': adj, 'L0_gnn_Wq': _L0_gnn_in['Wq'], 'L0_gnn_bq': _L0_gnn_in['bq'], 'L0_gnn_Wk': _L0_gnn_in['Wk'], 'L0_gnn_bk': _L0_gnn_in['bk'], 'L0_gnn_Wv': _L0_gnn_in['Wv'], 'L0_gnn_bv': _L0_gnn_in['bv'], 'L0_gnn_Wo': _L0_gnn_in['Wo'], 'L0_gnn_bo': _L0_gnn_in['bo'], 'L0_gnn_gamma': _L0_gnn_in['gamma'], 'L0_gnn_beta': _L0_gnn_in['beta'], 'L1_gnn_ln1_g': _L1_gnn_in['ln1_g'], 'L1_gnn_ln1_b': _L1_gnn_in['ln1_b'], 'L1_gnn_ln2_g': _L1_gnn_in['ln2_g'], 'L1_gnn_ln2_b': _L1_gnn_in['ln2_b'], 'L1_gnn_wq': _L1_gnn_in['wq'], 'L1_gnn_bq': _L1_gnn_in['bq'], 'L1_gnn_wk': _L1_gnn_in['wk'], 'L1_gnn_bk': _L1_gnn_in['bk'], 'L1_gnn_wv': _L1_gnn_in['wv'], 'L1_gnn_bv': _L1_gnn_in['bv'], 'L1_gnn_wo': _L1_gnn_in['wo'], 'L1_gnn_bo': _L1_gnn_in['bo'], 'L1_gnn_w1': _L1_gnn_in['w1'], 'L1_gnn_b1': _L1_gnn_in['b1'], 'L1_gnn_w2': _L1_gnn_in['w2'], 'L1_gnn_b2': _L1_gnn_in['b2']}

def reference(x, adj, L0_gnn_Wq, L0_gnn_bq, L0_gnn_Wk, L0_gnn_bk, L0_gnn_Wv, L0_gnn_bv, L0_gnn_Wo, L0_gnn_bo, L0_gnn_gamma, L0_gnn_beta, L1_gnn_ln1_g, L1_gnn_ln1_b, L1_gnn_ln2_g, L1_gnn_ln2_b, L1_gnn_wq, L1_gnn_bq, L1_gnn_wk, L1_gnn_bk, L1_gnn_wv, L1_gnn_bv, L1_gnn_wo, L1_gnn_bo, L1_gnn_w1, L1_gnn_b1, L1_gnn_w2, L1_gnn_b2):
    import jax
    import jax.numpy as jnp

    def _L0_gnn_ref(x, adj, Wq, bq, Wk, bk, Wv, bv, Wo, bo, gamma, beta):
        import jax, jax.numpy as jnp
        import numpy as np
        B, N, D, H = (4, 1024, 256, 8)
        HD = D // H
        EPS = 1e-05
        b, n, d = x.shape
        scale = 1.0 / np.sqrt(HD).astype(np.float32)
        q = (x @ Wq + bq).reshape(b, n, H, HD)
        k = (x @ Wk + bk).reshape(b, n, H, HD)
        v = (x @ Wv + bv).reshape(b, n, H, HD)
        scores = jnp.einsum('bnhd,bmhd->bhnm', q, k) * scale
        mask = (adj == 0)[:, None, :, :]
        scores = jnp.where(mask, jnp.float32(-jnp.inf), scores)
        attn = jax.nn.softmax(scores, axis=-1)
        h = jnp.einsum('bhnm,bmhd->bnhd', attn, v).reshape(b, n, d)
        h = h @ Wo + bo
        y = h + x
        mu = jnp.mean(y, axis=-1, keepdims=True)
        var = jnp.mean(jnp.square(y - mu), axis=-1, keepdims=True)
        return (y - mu) * jax.lax.rsqrt(var + EPS) * gamma + beta

    def _L1_gnn_ref(x, adj_matrix, edge_attr_matrix, ln1_g, ln1_b, ln2_g, ln2_b, wq, bq, wk, bk, wv, bv, wo, bo, w1, b1, w2, b2):
        import jax, jax.numpy as jnp
        import numpy as np
        B, S, D, H = (2, 1024, 256, 8)
        HD = D // H
        EPS = 1e-05

        def _ln(x, g, b):
            mu = jnp.mean(x, axis=-1, keepdims=True)
            var = jnp.mean((x - mu) ** 2, axis=-1, keepdims=True)
            return (x - mu) * jax.lax.rsqrt(var + EPS) * g + b
        b, s, d = x.shape
        residual = x
        nx = _ln(x, ln1_g, ln1_b)
        q = (nx @ wq + bq).reshape(b, s, H, HD).transpose(0, 2, 1, 3)
        k = (nx @ wk + bk).reshape(b, s, H, HD).transpose(0, 2, 1, 3)
        v = (nx @ wv + bv).reshape(b, s, H, HD).transpose(0, 2, 1, 3)
        adjf = adj_matrix.astype(jnp.float32)
        bias = jnp.where(adj_matrix > 0, 0.1 * edge_attr_matrix * adjf, -jnp.inf)[:, None]
        scores = jnp.einsum('bhqd,bhkd->bhqk', q, k) / np.sqrt(HD) + bias
        attn = jax.nn.softmax(scores, axis=-1)
        out = jnp.einsum('bhqk,bhkd->bhqd', attn, v)
        out = out.transpose(0, 2, 1, 3).reshape(b, s, d)
        x1 = residual + (out @ wo + bo)
        n2 = _ln(x1, ln2_g, ln2_b)
        mlp = jax.nn.gelu(n2 @ w1 + b1, approximate=False) @ w2 + b2
        return x1 + mlp
    x = _L0_gnn_ref(x, adj, L0_gnn_Wq, L0_gnn_bq, L0_gnn_Wk, L0_gnn_bk, L0_gnn_Wv, L0_gnn_bv, L0_gnn_Wo, L0_gnn_bo, L0_gnn_gamma, L0_gnn_beta)
    x = _L1_gnn_ref(x, adj, adj, L1_gnn_ln1_g, L1_gnn_ln1_b, L1_gnn_ln2_g, L1_gnn_ln2_b, L1_gnn_wq, L1_gnn_bq, L1_gnn_wk, L1_gnn_bk, L1_gnn_wv, L1_gnn_bv, L1_gnn_wo, L1_gnn_bo, L1_gnn_w1, L1_gnn_b1, L1_gnn_w2, L1_gnn_b2)
    return x

_drawn_inputs = setup_inputs


def setup_inputs(seed=0):
    import zlib

    import numpy as np

    out = dict(_drawn_inputs(seed))
    spreads = {'L0_gnn_bq': (0.0, 0.8),
     'L0_gnn_bk': (0.0, 0.8),
     'L0_gnn_bv': (0.0, 0.1),
     'L0_gnn_bo': (0.0, 0.1),
     'L0_gnn_gamma': (1.0, 0.2),
     'L0_gnn_beta': (0.0, 0.1),
     'L1_gnn_ln1_g': (1.0, 0.2),
     'L1_gnn_ln1_b': (0.0, 0.1),
     'L1_gnn_ln2_g': (1.0, 0.2),
     'L1_gnn_ln2_b': (0.0, 0.1),
     'L1_gnn_bq': (0.0, 0.1),
     'L1_gnn_bk': (0.0, 0.8),
     'L1_gnn_bv': (0.0, 0.1),
     'L1_gnn_bo': (0.0, 0.1),
     'L1_gnn_b1': (0.0, 0.1),
     'L1_gnn_b2': (0.0, 0.1)}
    factors = {}
    for name, (base, spread) in spreads.items():
        noise = np.random.default_rng([zlib.crc32(name.encode()), seed]).standard_normal(out[name].shape)
        drawn = base * np.exp(spread * noise) if base else spread * noise
        out[name] = jnp.asarray(drawn.astype(out[name].dtype))
    for name, factor in factors.items():
        out[name] = (out[name] * factor).astype(out[name].dtype)
    return out
```

```python
import math
from contextlib import ExitStack

import numpy as np

import concourse.bass as bass
from concourse import mybir

F32 = mybir.dt.float32
F32R = mybir.dt.float32r
I32 = mybir.dt.int32
ALU = mybir.AluOpType
ACT = mybir.ActivationFunctionType

B, N, D, H = 128, 128, 256, 8
HD = D // H
F = 4 * D
G = 4
T = G * N
NB = B // G
P = 128
C = D // P
HC = H // C
FC = F // P
SCALE = 1.0 / math.sqrt(HD)
EPS = 1e-5
BIG = 1e30
X, Y = 0, 1

JOBS = [("T1", -1, C), ("WO1", -2, 2), ("QKV1", -1, 6), ("T2", -2, C), ("MLP1", -2, FC),
        ("WO0", 0, 2), ("QKV0", 1, 6), ("MLP2", -2, 2)]
BANKS = 3
FIRST_FULL, LAST_FULL = 3, NB - 2


def exists(b):
    return 0 <= b < NB if isinstance(b, int) else True


def positions():
    at, out = 0, {}
    for name, off, n in JOBS:
        out[name] = at
        at += n
    return out


POS = positions()
ALL_JOBS = [off for _, off, n in JOBS for _ in range(n)]
PER_BANK = len(ALL_JOBS) // BANKS
assert len(ALL_JOBS) % BANKS == 0


def uses_before(i, pos):
    def count(it):
        same = range(pos % BANKS, len(ALL_JOBS), BANKS)
        n = sum(exists(k + ALL_JOBS[q]) for k in range(-1, it) for q in same)
        return n + sum(exists(it + ALL_JOBS[q]) for q in same if q < pos)
    if isinstance(i, int):
        return count(i)
    return i * PER_BANK + (count(FIRST_FULL) - FIRST_FULL * PER_BANK)


def slot(i, phase, g):
    if isinstance(i, int):
        if phase == X:
            return g if i == 0 else 8 * i - G + g
        return 8 * i + g if i < NB else 8 * i - G + g
    return i * 8 + (g - G if phase == X else g)


def program(nc, x, xT, adj, w):
    ctx = ExitStack()
    with ctx:
        def sb(name, shape, dt=F32):
            return ctx.enter_context(nc.sbuf_tensor(name, shape, dt))

        def bank(name):
            return ctx.enter_context(nc.psum_tensor(name, [P, 512], F32))

        def sem(name):
            return ctx.enter_context(nc.semaphore(name))

        wqkv = [[sb(f"wqkv{l}{p}", [P, C, 3 * D], F32R) for p in "hl"] for l in (0, 1)]
        wo = [[sb(f"wo{l}{p}", [P, C, D], F32R) for p in "hl"] for l in (0, 1)]
        w1 = [sb(f"w1{p}", [P, C, F], F32R) for p in "hl"]
        w2 = [sb(f"w2{p}", [P, FC, D], F32R) for p in "hl"]
        ident = sb("ident", [P, P])
        par = sb("par", [P, 10 * C + FC])
        cols = par[:, 0:8 * C].rearrange("p (n c) -> p n c", c=C)
        lnp = par[:, 8 * C:10 * C].rearrange("p (n c) -> p n c", c=C)
        b1raw = par[:, 10 * C:]
        nbq = sb("nbq", [P, 2, C])
        bk = sb("bk", [P, 2, C])
        bv = sb("bv", [P, 2, C])
        b1 = sb("b1", [P, FC])
        gamma = sb("gamma", [P, D])
        beta = sb("beta", [P, D])
        bo = [sb(f"bo{l}", [P, D]) for l in (0, 1)]
        b2 = sb("b2", [P, D])
        ones = sb("ones", [P, P])
        bvw = sb("bvw", [P, 2, C, P])
        power = sb("power", [P, G])
        xy = sb("xy", [P, G, D])
        xTr = sb("xTr", [P, C, T])
        act = [sb(f"act{p}", [P, C, T], F32R) for p in "hl"]
        q = [sb(f"q{l}", [P, C, T]) for l in (0, 1)]
        kp = [sb(f"kp{l}", [P, C, HC, T]) for l in (0, 1)]
        v = [sb(f"v{l}", [P, G, D]) for l in (0, 1)]
        ot = [sb(f"ot{p}", [P, C, T], F32R) for p in "hl"]
        y0 = sb("y0", [P, G, D])
        r1 = sb("r1", [P, G, D])
        x1 = sb("x1", [P, G, D])
        xh2 = sb("xh2", [P, G, D])
        hf = sb("hf", [P, 2, T])
        hh = [sb(f"h{p}", [P, FC, T], F32R) for p in "hl"]
        m0 = sb("m0", [P, G, N])
        a1 = sb("a1", [P, G, N])
        m1 = sb("m1", [P, G, N])
        pm = sb("pm", [P, 2, H, N])
        pt = sb("pt", [P, H, N])
        nmax = sb("nmax", [P, 2, H])
        rsum = sb("rsum", [P, 2, H])
        rinv = sb("rinv", [P, 2, H])
        stats = sb("stats", [P, 3, G, 6])
        mv = sb("mv", [P, 3, G, 2])
        veps = sb("veps", [P, 3, G])
        rstd = sb("rstd", [P, 3, G])

        ps_s = [bank("ps_s0"), bank("ps_s1")]
        ps_t = [bank("ps_t0"), bank("ps_t1")]
        ps_o = bank("ps_o")
        ps_j = [bank(f"ps_j{n}") for n in range(BANKS)]

        raw_loaded, par_loaded = sem("raw_loaded"), sem("par_loaded")
        x_loaded, xT_loaded, adj0_loaded, adj1_loaded = (
            sem("x_loaded"), sem("xT_loaded"), sem("adj0_loaded"), sem("adj1_loaded"))
        out_stored = sem("out_stored")
        ident_done, prep_split, prep_pe, prep_step, prep_act, prep_zero = (
            sem("ident_done"), sem("prep_split"), sem("prep_pe"), sem("prep_step"),
            sem("prep_act"), sem("prep_zero"))
        job_full = [sem(f"job_full{n}") for n in range(BANKS)]
        job_free = [sem(f"job_free{n}") for n in range(BANKS)]
        scores_full, masked, exp_done, rinv_done, norm_done = (
            sem("scores_full"), sem("masked"), sem("exp_done"), sem("rinv_done"), sem("norm_done"))
        pt_full, pt_a, pt_b, pv_done, ot_hi, ot_lo = (
            sem("pt_full"), sem("pt_a"), sem("pt_b"), sem("pv_done"), sem("ot_hi"), sem("ot_lo"))
        act_hi = [sem(f"act_hi{n}") for n in range(3)]
        act_lo0 = sem("act_lo0")
        mask0_done, mask1_done, mask1_step = sem("mask0_done"), sem("mask1_done"), sem("mask1_step")
        xb_done = sem("xb_done")
        y0_mul, y0_done, r1_done, x1b_done = (
            sem("y0_mul"), sem("y0_done"), sem("r1_done"), sem("x1b_done"))
        stats_done = [sem(f"stats_done{n}") for n in range(3)]
        aggr_done = [sem(f"aggr_done{n}") for n in range(3)]
        veps_done = [sem(f"veps_done{n}") for n in range(3)]
        rstd_done = [sem(f"rstd_done{n}") for n in range(3)]
        xhat_done = [sem(f"xhat_done{n}") for n in range(3)]
        h_hi, h_lo = sem("h_hi"), sem("h_lo")
        tick, carried = sem("tick"), sem("carried")

        def need(eng, s, n):
            if not isinstance(n, int) or n > 0:
                eng.wait_ge(s, n)

        def filled(eng, i, pos):
            eng.wait_ge(job_full[pos % BANKS], uses_before(i, pos) + 1)
            return ps_j[pos % BANKS]

        def taken(eng, i, *places):
            for pos in places:
                eng.wait_ge(job_free[pos % BANKS], uses_before(i, pos) + 1)

        def iterate(eng, body):
            for i in range(-1, FIRST_FULL):
                body(i)
            with eng.Fori(FIRST_FULL, LAST_FULL + 1) as i:
                body(i)
            for i in range(LAST_FULL + 1, NB + 2):
                body(i)

        def act_read(eng, i):
            for off, at, pos in ((-2, i, POS["MLP1"] + FC - 1), (-1, i, POS["QKV1"] + 5), (0, i - 1, POS["QKV0"] + 5)):
                if exists(i + off):
                    filled(eng, at, pos)
                    return

        raw0 = kp[0][:, :, :, :].rearrange("p c h t -> p (c h t)")
        raw1 = kp[1][:, :, :, :].rearrange("p c h t -> p (c h t)")
        raw_qkv = [raw0[:, l * 6 * D:(l + 1) * 6 * D].rearrange("p (c n) -> p c n", c=C) for l in (0, 1)]
        raw_o = [raw0[:, (12 + 2 * l) * D:(14 + 2 * l) * D].rearrange("p (c n) -> p c n", c=C)
                 for l in (0, 1)]
        raw_1 = raw1[:, 0:C * F].rearrange("p (c n) -> p c n", c=C)
        raw_2 = raw1[:, C * F:C * F + FC * D].rearrange("p (c n) -> p c n", c=FC)
        BQ, BK, BV, LG, LB = 0, 2, 4, 6, 7

        block = ctx.enter_context(nc.Block())

        @block.sync
        def _(sp):
            x_b = x.rearrange("(b g) t f -> b t g f", g=G)
            a_b = adj.rearrange("(b g) q k -> b q g k", g=G)
            o_b = w["out"].rearrange("(b g) t f -> b t g f", g=G)
            xT_v = xT.rearrange("(c p) n -> p c n", p=P)

            def row(name):
                return w[name].rearrange("(a n) -> a n", a=1).to_broadcast([P, D])

            for l in (0, 1):
                for n, part in enumerate(("q", "k", "v")):
                    sp.dma_start(raw_qkv[l][:, :, n * D:(n + 1) * D],
                                 w[f"w{part}{l}"].rearrange("(c p) n -> p c n", p=P)).then_inc(raw_loaded, 16)
            for l in (0, 1):
                sp.dma_start(raw_o[l], w[f"wo{l}"].rearrange("(c p) n -> p c n", p=P)).then_inc(raw_loaded, 16)
            sp.dma_start(raw_1, w["w1"].rearrange("(c p) n -> p c n", p=P)).then_inc(raw_loaded, 16)
            sp.dma_start(raw_2, w["w2"].rearrange("(c p) n -> p c n", p=P)).then_inc(raw_loaded, 16)
            sp.dma_start(par[:, :], w["columns"]).then_inc(par_loaded, 16)
            for dst, name in ((gamma, "gamma"), (beta, "beta"), (bo[0], "bo0"), (bo[1], "bo1"), (b2, "b2")):
                sp.dma_start(dst[:, :], row(name)).then_inc(par_loaded, 16)

            def body(i):
                if exists(i + 1):
                    need(sp, act_hi[0], 2 * (i + 1))
                    need(sp, act_lo0, 2 * (i + 1))
                    sp.dma_start(xTr[:, :, :], xT_v[:, :, bass.ts(i + 1, T)]).then_inc(xT_loaded, 16)
                if exists(i):
                    if exists(i - 1):
                        filled(sp, i, POS["T1"] + C - 1)
                    sp.dma_start(xy[:, :, :], x_b[bass.ds(i, 1), :, :, :].rearrange("a t g f -> t (a g) f")) \
                      .then_inc(x_loaded, 16)
                if exists(i):
                    need(sp, mask1_done, i)
                    sp.dma_start(a1[:, :, :].bitcast(I32),
                                 a_b[bass.ds(i, 1), :, :, :].rearrange("a q g k -> q (a g) k")) \
                      .then_inc(adj1_loaded, 16)
                if exists(i + 1):
                    if exists(i):
                        need(sp, masked, 2 * slot(i, X, G - 1) + 2)
                    sp.dma_start(m0[:, :, :].bitcast(I32),
                                 a_b[bass.ds(i + 1, 1), :, :, :].rearrange("a q g k -> q (a g) k")) \
                      .then_inc(adj0_loaded, 16)
                if exists(i - 2):
                    taken(sp, i, POS["MLP2"], POS["MLP2"] + 1)
                    sp.dma_start(o_b[bass.ds(i - 2, 1), :, :, :].rearrange("a t g f -> t (a g) f"),
                                 x1[:, :, :]).then_inc(out_stored, 16)

            iterate(sp, body)
            sp.wait_ge(out_stored, 16 * NB)

        @block.tensor
        def _(pe):
            mm = nc.tensor.matmul

            pe.wait_ge(raw_loaded, 16 * 10)
            pe.wait_ge(par_loaded, 16 * 6)
            for n in range(3 * C):
                for c in range(C):
                    last = mm(ps_j[0][:, n:n + 1], raw_qkv[1][:, c, n * P:(n + 1) * P],
                              cols[:, LB, c:c + 1], start=(c == 0), stop=(c == C - 1))
            for m in range(FC):
                for c in range(C):
                    last = mm(ps_j[0][:, 3 * C + m:3 * C + m + 1], raw_1[:, c, m * P:(m + 1) * P],
                              lnp[:, 1, c:c + 1], start=(c == 0), stop=(c == C - 1))
            last.then_inc(prep_pe, 1)
            pe.wait_ge(prep_step, 3)
            for l in (0, 1):
                for c in range(C):
                    last = mm(ps_j[1 + l][:, 0:D], bvw[:, l, c, :], raw_o[l][:, c, :],
                              start=(c == 0), stop=(c == C - 1))
            last.then_inc(prep_pe, 1)
            pe.wait_ge(prep_split, 1)
            pe.wait_ge(prep_act, 2)
            pe.wait_ge(ident_done, 3)

            def open_job(i, pos):
                need(pe, job_free[pos % BANKS], uses_before(i, pos))
                return ps_j[pos % BANKS]

            def scores(i, phase, g):
                l, n = phase, slot(i, phase, g)
                if g == 0:
                    taken(pe, i - 1 if phase == X else i, *(POS[f"QKV{l}"] + m for m in range(3, 6)))
                for c in range(C):
                    need(pe, masked, 2 * n - C + c + 1)
                    mm(ps_s[c][:, :].rearrange("p (h k) -> p h k", h=HC), q[l][:, c, g * N:(g + 1) * N],
                       kp[l][:, c, :, g * N:(g + 1) * N], start=True, stop=True).then_inc(scores_full, 1)

            def flip(i, phase, g):
                n = slot(i, phase, g)
                for c in range(C):
                    need(pe, norm_done, 2 * n + c + 1)
                    need(pe, (pt_a, pt_b)[c], n)
                    for j in range(HC):
                        last = nc.tensor.transpose(ps_t[c][:, j * N:(j + 1) * N],
                                                   pm[:, g % 2, c * HC + j, :], ident[:, :])
                    last.then_inc(pt_full, 1)

            def values(i, phase, g):
                l, n = phase, slot(i, phase, g)
                need(pe, pt_a, n + 1)
                need(pe, pt_b, n + 1)
                need(pe, ot_lo, n)
                for h in range(H):
                    j = h % HC
                    last = mm(ps_o[j * HD:(j + 1) * HD, (h // HC) * N:(h // HC + 1) * N],
                              v[l][:, g, h * HD:(h + 1) * HD], pt[:, h, :], start=True, stop=True)
                last.then_inc(pv_done, 1)

            def split_mm(out, parts, wparts, pick, wpick, chunks):
                terms = [(c, a, b) for c in range(chunks) for a, b in ((0, 0), (0, 1), (1, 0))]
                for n, (c, a, b) in enumerate(terms):
                    last = mm(out, pick(parts[a], c), wpick(wparts[b], c),
                              start=(n == 0), stop=(n == len(terms) - 1))
                return last

            def flip_rows(i, name, off, src, k):
                if exists(i + off):
                    need(pe, xhat_done[k], i + off + 1)
                    for c in range(C):
                        pos = POS[name] + c
                        out = open_job(i, pos)
                        for g in range(G):
                            last = nc.tensor.transpose(out[:, g * N:(g + 1) * N],
                                                       src[:, g, c * P:(c + 1) * P], ident[:, :])
                        last.then_inc(job_full[pos % BANKS], 1)

            def out_proj(i, l, j):
                off = 0 if l == 0 else -2
                if not exists(i + off):
                    return
                pos = POS[f"WO{l}"] + j
                n = slot(i, X, 2 * j + 1) if l == 0 else slot(i - 1, Y, 2 * j + 1)
                need(pe, ot_lo, n + 1)
                out = open_job(i, pos)
                for g in (2 * j, 2 * j + 1):
                    last = split_mm(out[:, (g % 2) * D:(g % 2 + 1) * D], ot, wo[l],
                                    lambda t, c: t[:, c, g * N:(g + 1) * N], lambda t, c: t[:, c, :], C)
                last.then_inc(job_full[pos % BANKS], 1)

            def qkv(i, l, ns):
                b = i + (1 if l == 0 else -1)
                if not exists(b):
                    return
                for n in ns:
                    pos = POS[f"QKV{l}"] + n
                    if n == 0 and l == 0:
                        need(pe, act_hi[0], C * (b + 1))
                        need(pe, act_lo0, C * (b + 1))
                    elif n == 0:
                        taken(pe, i, POS["T1"], POS["T1"] + 1)
                    out = open_job(i, pos)
                    if n < 4:
                        last = split_mm(out[:, :], wqkv[l], act,
                                        lambda t, c: t[:, c, n * P:(n + 1) * P], lambda t, c: t[:, c, :], C)
                    else:
                        for g in (2 * (n - 4), 2 * (n - 4) + 1):
                            last = split_mm(out[:, (g % 2) * D:(g % 2 + 1) * D], act, wqkv[l],
                                            lambda t, c: t[:, c, g * N:(g + 1) * N],
                                            lambda t, c: t[:, c, 2 * D:3 * D], C)
                    last.then_inc(job_full[pos % BANKS], 1)

            def mlp_up(i, m):
                b = i - 2
                if not exists(b):
                    return
                pos = POS["MLP1"] + m
                if m == 0:
                    taken(pe, i, POS["T2"], POS["T2"] + 1)
                out = open_job(i, pos)
                split_mm(out[:, :], w1, act, lambda t, c: t[:, c, m * P:(m + 1) * P],
                         lambda t, c: t[:, c, :], C).then_inc(job_full[pos % BANKS], 1)

            def mlp_down(i, g):
                b = i - 2
                if not exists(b):
                    return
                pos = POS["MLP2"] + g // 2
                out = ps_j[pos % BANKS]
                if g % 2 == 0:
                    need(pe, h_lo, FC * (b + 1))
                    open_job(i, pos)
                last = split_mm(out[:, (g % 2) * D:(g % 2 + 1) * D], hh, w2,
                                lambda t, c: t[:, c, g * N:(g + 1) * N], lambda t, c: t[:, c, :], FC)
                if g % 2 == 1:
                    last.then_inc(job_full[pos % BANKS], 1)

            def body(i):
                on = exists(i)
                if on:
                    scores(i, X, 0)
                flip_rows(i, "T1", -1, xy, 1)
                out_proj(i, 1, 0)
                out_proj(i, 1, 1)
                if on:
                    scores(i, X, 1)
                qkv(i, 1, (0, 1, 2))
                if on:
                    flip(i, X, 0)
                    scores(i, X, 2)
                qkv(i, 1, (3, 4, 5))
                if on:
                    values(i, X, 0)
                    flip(i, X, 1)
                    scores(i, X, 3)
                    values(i, X, 1)
                    flip(i, X, 2)
                flip_rows(i, "T2", -2, xh2, 2)
                mlp_up(i, 0)
                mlp_up(i, 1)
                if on:
                    values(i, X, 2)
                mlp_up(i, 2)
                mlp_up(i, 3)
                if on:
                    flip(i, X, 3)
                mlp_up(i, 4)
                mlp_up(i, 5)
                if on:
                    values(i, X, 3)
                mlp_up(i, 6)
                mlp_up(i, 7)

                on = exists(i - 1)
                if on:
                    scores(i, Y, 0)
                out_proj(i, 0, 0)
                out_proj(i, 0, 1)
                if on:
                    scores(i, Y, 1)
                qkv(i, 0, (0, 1, 2))
                if on:
                    flip(i, Y, 0)
                    scores(i, Y, 2)
                qkv(i, 0, (3, 4, 5))
                if on:
                    values(i, Y, 0)
                    flip(i, Y, 1)
                    scores(i, Y, 3)
                    values(i, Y, 1)
                    flip(i, Y, 2)
                mlp_down(i, 0)
                if on:
                    values(i, Y, 2)
                mlp_down(i, 1)
                if on:
                    flip(i, Y, 3)
                mlp_down(i, 2)
                if on:
                    values(i, Y, 3)
                mlp_down(i, 3)

            iterate(pe, body)

        @block.scalar
        def _(sc):
            sc.wait_ge(prep_step, 2)
            nc.scalar.activation(nbq[:, :, :], cols[:, BQ:BQ + 2, :], ACT.Copy, scale=-SCALE).then_inc(prep_act, 1)
            nc.scalar.activation(bk[:, :, :], cols[:, BK:BK + 2, :], ACT.Copy).then_inc(prep_act, 1)
            sc.wait_ge(prep_act, 2)
            sc.wait_ge(prep_zero, 2)

            def exp(i, phase, g):
                n = slot(i, phase, g)
                for h in range(H):
                    if h % HC == 0:
                        need(sc, masked, 2 * n + h // HC + 1)
                    last = nc.scalar.activation(pm[:, g % 2, h, :], pm[:, g % 2, h, :], ACT.Exp,
                                                bias=nmax[:, g % 2, h:h + 1], scale=-1.0,
                                                accum_out=rsum[:, g % 2, h:h + 1])
                    if h % HC == HC - 1:
                        last.then_inc(exp_done, 1)

            def copy_pt(i, phase, g):
                n = slot(i, phase, g)
                need(sc, pt_full, 2 * n + 1)
                nc.scalar.activation(pt[:, 0:HC, :], ps_t[0][:, :].rearrange("p (h q) -> p h q", h=HC),
                                     ACT.Copy).then_inc(pt_a, 1)

            def out_hi(i, phase, g):
                n = slot(i, phase, g)
                need(sc, pv_done, n + 1)
                nc.scalar.activation(ot[0][:, :, g * N:(g + 1) * N],
                                     ps_o[:, 0:C * N].rearrange("p (c q) -> p c q", c=C),
                                     ACT.Copy).then_inc(ot_hi, 1)

            def qk_out(i, l, ns):
                b = i + (1 if l == 0 else -1)
                if not exists(b):
                    return
                for n in ns:
                    pos = POS[f"QKV{l}"] + n
                    src = filled(sc, i, pos)
                    c = n % C
                    if n < 2:
                        nc.scalar.activation(q[l][:, c, :], src[:, :], ACT.Identity,
                                             bias=nbq[:, l, c:c + 1], scale=-SCALE).then_inc(job_free[pos % BANKS], 1)
                    else:
                        for j in range(HC):
                            rows = slice(j * HD, (j + 1) * HD)
                            last = nc.scalar.activation(kp[l][rows, c, j, :], src[rows, :], ACT.Identity,
                                                        bias=bk[rows, l, c:c + 1])
                        last.then_inc(job_free[pos % BANKS], 1)

            def hi(i, name, off, k):
                if exists(i + off):
                    for c in range(C):
                        pos = POS[name] + c
                        src = filled(sc, i, pos)
                        nc.scalar.activation(act[0][:, c, :], src[:, :], ACT.Copy).then_inc(act_hi[k], 1)

            def gelu(i, ms):
                b = i - 2
                if not exists(b):
                    return
                for m in ms:
                    pos = POS["MLP1"] + m
                    src = filled(sc, i, pos)
                    need(sc, h_lo, FC * b + m - 1)
                    nc.scalar.activation(hf[:, m % 2, :], src[:, :], ACT.Gelu,
                                         bias=b1[:, m:m + 1]).then_inc(job_free[pos % BANKS], 1)

            def body(i):
                on = exists(i)
                hi(i, "T1", -1, 1)
                if on:
                    exp(i, X, 0)
                qk_out(i, 1, (0, 1))
                if on:
                    exp(i, X, 1)
                qk_out(i, 1, (2,))
                if on:
                    copy_pt(i, X, 0)
                qk_out(i, 1, (3,))
                if on:
                    exp(i, X, 2)
                    out_hi(i, X, 0)
                    copy_pt(i, X, 1)
                    out_hi(i, X, 1)
                    copy_pt(i, X, 2)
                    exp(i, X, 3)
                hi(i, "T2", -2, 2)
                if on:
                    out_hi(i, X, 2)
                gelu(i, (0, 1, 2))
                if on:
                    copy_pt(i, X, 3)
                gelu(i, (3, 4, 5))
                if on:
                    out_hi(i, X, 3)
                gelu(i, (6, 7))

                on = exists(i - 1)
                if exists(i + 1):
                    need(sc, xT_loaded, 16 * (i + 2))
                    act_read(sc, i)
                    for c in range(C):
                        nc.scalar.activation(act[0][:, c, :], xTr[:, c, :], ACT.Copy).then_inc(act_hi[0], 1)
                if on:
                    exp(i, Y, 0)
                qk_out(i, 0, (0, 1))
                if on:
                    exp(i, Y, 1)
                qk_out(i, 0, (2,))
                if on:
                    copy_pt(i, Y, 0)
                qk_out(i, 0, (3,))
                if on:
                    exp(i, Y, 2)
                    out_hi(i, Y, 0)
                    copy_pt(i, Y, 1)
                    out_hi(i, Y, 1)
                    copy_pt(i, Y, 2)
                    exp(i, Y, 3)
                    out_hi(i, Y, 2)
                    copy_pt(i, Y, 3)
                    out_hi(i, Y, 3)

            iterate(sc, body)

        @block.vector
        def _(dve):
            tt, ts = nc.vector.tensor_tensor, nc.vector.tensor_scalar

            dve.wait_ge(raw_loaded, 16 * 10)
            dve.wait_ge(par_loaded, 16 * 6)
            nc.vector.memset(ones[:, :], 1.0)
            nc.vector.memset(power[:, :], -0.5)
            parts = []
            for c in range(C):
                parts += [(wqkv[0][0][:, c, :], wqkv[0][1][:, c, :], raw_qkv[0][:, c, :], 1.0),
                          (wqkv[1][0][:, c, :], wqkv[1][1][:, c, :], raw_qkv[1][:, c, :], cols[:, LG, c:c + 1]),
                          (w1[0][:, c, :], w1[1][:, c, :], raw_1[:, c, :], lnp[:, 0, c:c + 1])]
            for l in (0, 1):
                parts.append((wo[l][0][:, :, :], wo[l][1][:, :, :], raw_o[l], 1.0))
            for k in range(2):
                half = slice(k * FC // 2, (k + 1) * FC // 2)
                parts.append((w2[0][:, half, :], w2[1][:, half, :], raw_2[:, half, :], 1.0))
            for k, (h, _, raw, by) in enumerate(parts):
                ts(h, raw, by, None, ALU.mult).then_inc(tick, 1)
            dve.wait_ge(tick, len(parts))
            for k, (h, lo, raw, by) in enumerate(parts):
                nc.vector.scalar_tensor_tensor(lo, raw, by, h.bitcast(F32), ALU.mult, ALU.subtract)\
                  .then_inc(tick, 1)
            dve.wait_ge(prep_pe, 1)
            shifts = ps_j[0][:, 0:3 * C + FC]
            for n, to in ((0, BQ + 1), (1, BK + 1), (2, BV + 1)):
                last = tt(cols[:, to, :], cols[:, to, :], shifts[:, n * C:(n + 1) * C], ALU.add)
            last.then_inc(prep_step, 1)
            tt(b1[:, :], b1raw, shifts[:, 3 * C:], ALU.add).then_inc(prep_step, 1)
            dve.wait_ge(prep_step, 2)
            for l in (0, 1):
                for c in range(C):
                    last = ts(bvw[:, l, c, :], ones[:, :], cols[:, BV + l, c:c + 1], None, ALU.mult)
            last.then_inc(prep_step, 1)
            dve.wait_ge(prep_pe, 2)
            for l in (0, 1):
                last = tt(bo[l][:, :], bo[l][:, :], ps_j[1 + l][:, 0:D], ALU.add)
            last.then_inc(prep_step, 1)
            dve.wait_ge(tick, 2 * len(parts))
            for l in (0, 1):
                nc.vector.memset(kp[l][:, :, :, :], 0.0).then_inc(prep_zero, 1)
            dve.wait_ge(prep_zero, 2)
            dve.sem_inc(prep_split, 1)

            def mask0(b):
                if exists(b):
                    dve.wait_ge(adj0_loaded, 16 * (b + 1))
                    ts(m0[:, :, :], m0[:, :, :].bitcast(I32), 0, BIG, ALU.is_equal, ALU.mult)\
                      .then_inc(mask0_done, 1)

            def mask1(b):
                if exists(b):
                    dve.wait_ge(adj1_loaded, 16 * (b + 1))
                    a = a1[:, :, :].bitcast(I32)
                    nc.vector.scalar_tensor_tensor(m1[:, :, :], a, -0.1, a, ALU.mult, ALU.mult)\
                      .then_inc(mask1_step, 1)
                    dve.wait_ge(mask1_step, 2 * b + 1)
                    ts(a1[:, :, :], a, 0, BIG, ALU.is_le, ALU.mult).then_inc(mask1_step, 1)
                    dve.wait_ge(mask1_step, 2 * b + 2)
                    tt(m1[:, :, :], m1[:, :, :], a1[:, :, :], ALU.add).then_inc(mask1_done, 1)

            def mask_scores(i, phase, g):
                n = slot(i, phase, g)
                if g == 0:
                    dve.wait_ge((mask0_done, mask1_done)[phase], (i if phase == X else i - 1) + 1)
                m = (m0, m1)[phase]
                for h in range(H):
                    if h % HC == 0:
                        dve.wait_ge(scores_full, 2 * n + h // HC + 1)
                        dve.sem_inc(carried, 1)
                    last = nc.vector.tensor_tensor_reduce(
                        out=pm[:, g % 2, h, :], in0=ps_s[h // HC][:, (h % HC) * N:(h % HC + 1) * N],
                        in1=m[:, g, :], scale=1.0, scalar=3e38, op0=ALU.add, op1=ALU.min,
                        accum_out=nmax[:, g % 2, h:h + 1])
                    if h % HC == HC - 1:
                        last.then_inc(masked, 1)

            def recip(i, phase, g):
                n = slot(i, phase, g)
                dve.wait_ge(exp_done, 2 * n + 2)
                nc.vector.reciprocal(rinv[:, g % 2, :], rsum[:, g % 2, :]).then_inc(rinv_done, 1)

            def copy_pt(i, phase, g):
                n = slot(i, phase, g)
                dve.wait_ge(pt_full, 2 * n + 2)
                nc.vector.tensor_copy(pt[:, HC:H, :], ps_t[1][:, :].rearrange("p (h q) -> p h q", h=HC))\
                  .then_inc(pt_b, 1)

            def out_lo(i, phase, g):
                n = slot(i, phase, g)
                dve.wait_ge(ot_hi, n + 1)
                cols_g = slice(g * N, (g + 1) * N)
                tt(ot[1][:, :, cols_g], ps_o[:, 0:C * N].rearrange("p (c q) -> p c q", c=C),
                   ot[0][:, :, cols_g].bitcast(F32), ALU.subtract).then_inc(ot_lo, 1)

            def lo(i, name, off, k):
                b = i + off
                if exists(b):
                    for c in range(C):
                        pos = POS[name] + c
                        filled(dve, i, pos)
                        dve.wait_ge(act_hi[k], C * b + c + 1)
                        tt(act[1][:, c, :], ps_j[pos % BANKS][:, :], act[0][:, c, :].bitcast(F32),
                           ALU.subtract).then_inc(job_free[pos % BANKS], 1)

            def v_out(i, l):
                if exists(i + (1 if l == 0 else -1)):
                    for j in (0, 1):
                        pos = POS[f"QKV{l}"] + 4 + j
                        src = filled(dve, i, pos)
                        nc.vector.tensor_copy(v[l][:, 2 * j:2 * j + 2, :],
                                              src[:, :].rearrange("p (g n) -> p g n", g=2))\
                          .then_inc(job_free[pos % BANKS], 1)

            def residual(i, name, off, out, add, ready):
                b = i + off
                if exists(b):
                    ready(b)
                    for j in (0, 1):
                        pos = POS[name] + j
                        src = filled(dve, i, pos)
                        gs = slice(2 * j, 2 * j + 2)
                        tt(out[:, gs, :], src[:, :].rearrange("p (g n) -> p g n", g=2), add[:, gs, :],
                           ALU.add).then_inc(job_free[pos % BANKS], 1)

            def norm_stats(b, k, src, ready):
                if exists(b):
                    ready()
                    for g in range(G):
                        last = nc.vector.bn_stats(stats[:, k, g, :], src[:, g, :])
                    last.then_inc(stats_done[k], 1)
                    dve.wait_ge(stats_done[k], b + 1)
                    dve.sem_inc(carried, 1)
                    for g in range(G):
                        last = nc.vector.bn_aggr(mv[:, k, g, :], stats[:, k, g, :])
                    last.then_inc(aggr_done[k], 1)
                    dve.wait_ge(aggr_done[k], b + 1)
                    ts(veps[:, k, :], mv[:, k, :, 1], EPS, None, ALU.add).then_inc(veps_done[k], 1)

            def norm_rows(b, k, out, src):
                if exists(b):
                    dve.wait_ge(rstd_done[k], b + 1)
                    for g in range(G):
                        last = ts(out[:, g, :], src[:, g, :], mv[:, k, g, 0:1], rstd[:, k, g:g + 1],
                                  ALU.subtract, ALU.mult)
                    last.then_inc(xhat_done[k], 1)

            def split_h(i, ms):
                b = i - 2
                if exists(b):
                    for m in ms:
                        taken(dve, i, POS["MLP1"] + m)
                        nc.vector.tensor_copy(hh[0][:, m, :], hf[:, m % 2, :]).then_inc(h_hi, 1)
                        dve.wait_ge(h_hi, FC * b + m + 1)
                        tt(hh[1][:, m, :], hf[:, m % 2, :], hh[0][:, m, :].bitcast(F32),
                           ALU.subtract).then_inc(h_lo, 1)

            def body(i):
                on = exists(i)
                if on:
                    mask_scores(i, X, 0)
                lo(i, "T1", -1, 1)

                def res1_ready(b):
                    dve.wait_ge(r1_done, b + 1)
                    need(dve, out_stored, 16 * b)

                residual(i, "WO1", -2, x1, r1, res1_ready)
                norm_stats(i - 2, 2, x1, lambda: taken(dve, i, POS["WO1"], POS["WO1"] + 1))
                if on:
                    recip(i, X, 0)
                    mask_scores(i, X, 1)
                mask1(i - 1)
                norm_rows(i - 2, 2, xh2, x1)
                if on:
                    copy_pt(i, X, 0)
                    recip(i, X, 1)
                    mask_scores(i, X, 2)
                v_out(i, 1)
                if on:
                    recip(i, X, 2)
                    out_lo(i, X, 0)
                    copy_pt(i, X, 1)
                    mask_scores(i, X, 3)
                    out_lo(i, X, 1)
                    copy_pt(i, X, 2)
                    recip(i, X, 3)
                lo(i, "T2", -2, 2)
                if on:
                    out_lo(i, X, 2)
                split_h(i, (0, 1, 2))
                if on:
                    copy_pt(i, X, 3)
                split_h(i, (3, 4, 5))
                if on:
                    out_lo(i, X, 3)
                split_h(i, (6, 7))

                on = exists(i - 1)
                if exists(i + 1):
                    for c in range(C):
                        dve.wait_ge(act_hi[0], C * (i + 1) + c + 1)
                        tt(act[1][:, c, :], xTr[:, c, :], act[0][:, c, :].bitcast(F32), ALU.subtract)\
                          .then_inc(act_lo0, 1)
                if on:
                    mask_scores(i, Y, 0)
                residual(i, "WO0", 0, xy, xy, lambda b: dve.wait_ge(xb_done, b + 1))
                norm_stats(i, 0, xy, lambda: taken(dve, i, POS["WO0"], POS["WO0"] + 1))
                if on:
                    recip(i, Y, 0)
                    mask_scores(i, Y, 1)
                mask0(i + 1)
                norm_rows(i, 0, xy, xy)
                if on:
                    copy_pt(i, Y, 0)
                    recip(i, Y, 1)
                    mask_scores(i, Y, 2)
                v_out(i, 0)
                if on:
                    recip(i, Y, 2)
                    out_lo(i, Y, 0)
                    copy_pt(i, Y, 1)
                    mask_scores(i, Y, 3)
                norm_stats(i, 1, y0, lambda: dve.wait_ge(y0_done, i + 1))
                if on:
                    out_lo(i, Y, 1)
                    copy_pt(i, Y, 2)
                    recip(i, Y, 3)
                    out_lo(i, Y, 2)
                    copy_pt(i, Y, 3)
                norm_rows(i, 1, xy, y0)
                if on:
                    out_lo(i, Y, 3)
                residual(i, "MLP2", -2, x1, x1, lambda b: dve.wait_ge(x1b_done, b + 1))

            iterate(dve, body)

        @block.gpsimd
        def _(pool):
            tt = nc.gpsimd.tensor_tensor
            nc.gpsimd.memset(ident[:, :], 0.0).then_inc(ident_done, 1)
            pool.wait_ge(ident_done, 1)
            nc.gpsimd.affine_select(out=ident[:, :], in_=ident[:, :], compare_op=ALU.not_equal, fill=1.0,
                                    base=0, pattern=[[-1, P]], channel_multiplier=1).then_inc(ident_done, 2)
            pool.wait_ge(prep_step, 4)

            def over_rows(t):
                return t[:, :].rearrange("p (a n) -> p a n", a=1).to_broadcast([P, G, D])

            def normalise(i, phase, g):
                n = slot(i, phase, g)
                pool.wait_ge(rinv_done, n + 1)
                for c in range(C):
                    hs = slice(c * HC, (c + 1) * HC)
                    tt(pm[:, g % 2, hs, :], pm[:, g % 2, hs, :],
                       rinv[:, g % 2, hs].rearrange("p (h a) -> p h a", a=1).to_broadcast([P, HC, N]),
                       ALU.mult).then_inc(norm_done, 1)

            def root(b, k):
                if exists(b):
                    pool.wait_ge(veps_done[k], b + 1)
                    tt(rstd[:, k, :], veps[:, k, :], power[:, :], ALU.pow).then_inc(rstd_done[k], 1)

            def body(i):
                on = exists(i)
                if on:
                    normalise(i, X, 0)
                root(i - 2, 2)
                if exists(i - 1):
                    if exists(i - 2):
                        taken(pool, i, POS["WO1"], POS["WO1"] + 1)
                    pool.wait_ge(y0_done, i)
                    tt(r1[:, :, :], y0[:, :, :], over_rows(bo[1]), ALU.add).then_inc(r1_done, 1)
                if on:
                    normalise(i, X, 1)
                if exists(i - 2):
                    pool.wait_ge(xhat_done[2], i - 1)
                    tt(x1[:, :, :], x1[:, :, :], over_rows(b2), ALU.add).then_inc(x1b_done, 1)
                if on:
                    normalise(i, X, 2)
                    pool.wait_ge(x_loaded, 16 * (i + 1))
                    tt(xy[:, :, :], xy[:, :, :], over_rows(bo[0]), ALU.add).then_inc(xb_done, 1)
                    normalise(i, X, 3)

                on = exists(i - 1)
                if on:
                    normalise(i, Y, 0)
                root(i, 0)
                if on:
                    normalise(i, Y, 1)
                if exists(i):
                    pool.wait_ge(xhat_done[0], i + 1)
                    tt(y0[:, :, :], xy[:, :, :], over_rows(gamma), ALU.mult).then_inc(y0_mul, 1)
                    pool.wait_ge(y0_mul, i + 1)
                    tt(y0[:, :, :], y0[:, :, :], over_rows(beta), ALU.add).then_inc(y0_done, 1)
                if on:
                    normalise(i, Y, 2)
                root(i, 1)
                if on:
                    normalise(i, Y, 3)

            iterate(pool, body)


WEIGHTS = {
    "wq0": "L0_gnn_Wq", "bq0": "L0_gnn_bq", "wk0": "L0_gnn_Wk", "bk0": "L0_gnn_bk",
    "wv0": "L0_gnn_Wv", "bv0": "L0_gnn_bv", "wo0": "L0_gnn_Wo", "bo0": "L0_gnn_bo",
    "gamma": "L0_gnn_gamma", "beta": "L0_gnn_beta",
    "ln1_g": "L1_gnn_ln1_g", "ln1_b": "L1_gnn_ln1_b", "ln2_g": "L1_gnn_ln2_g", "ln2_b": "L1_gnn_ln2_b",
    "wq1": "L1_gnn_wq", "bq1": "L1_gnn_bq", "wk1": "L1_gnn_wk", "bk1": "L1_gnn_bk",
    "wv1": "L1_gnn_wv", "bv1": "L1_gnn_bv", "wo1": "L1_gnn_wo", "bo1": "L1_gnn_bo",
    "w1": "L1_gnn_w1", "b1": "L1_gnn_b1", "w2": "L1_gnn_w2", "b2": "L1_gnn_b2",
}

COLUMNS = ("bq0", "bq1", "bk0", "bk1", "bv0", "bv1", "ln1_g", "ln1_b", "ln2_g", "ln2_b", "b1")


def kernel(**inputs):
    import concourse.bacc as _bacc
    from concourse.bass_utils import run_bass_kernel_spmd as _run

    nc = _bacc.Bacc("TRN2", target_bir_lowering=False, num_devices=1, dynamic_dma_scratch_size=1024)
    x = np.ascontiguousarray(inputs["x"])
    arrays = {"x": x, "xT": np.ascontiguousarray(x.reshape(B * N, D).T),
              "adj": np.ascontiguousarray(inputs["adj"])}
    for short, name in WEIGHTS.items():
        if short not in COLUMNS:
            arrays[short] = np.ascontiguousarray(inputs[name])
    arrays["columns"] = np.ascontiguousarray(
        np.concatenate([inputs[WEIGHTS[short]].reshape(-1, P).T for short in COLUMNS], axis=1))
    arrays = {f"in_{k}": a for k, a in arrays.items()}
    aps = {k[3:]: nc.dram_tensor(k, a.shape, mybir.dt.from_np(a.dtype), kind="ExternalInput").ap()
           for k, a in arrays.items()}
    aps["out"] = nc.dram_tensor("out", (B, N, D), F32, kind="ExternalOutput").ap()
    program(nc, aps.pop("x"), aps.pop("xT"), aps.pop("adj"), aps)
    r = _run(nc, [arrays], core_ids=[0])
    return r.results[0]["out"]
```

```python
import math
from contextlib import ExitStack

import numpy as np

import concourse.bass as bass
from concourse import mybir

F32 = mybir.dt.float32
F32R = mybir.dt.float32r
I32 = mybir.dt.int32
ALU = mybir.AluOpType
ACT = mybir.ActivationFunctionType

B, N, D, H = 128, 128, 256, 8
HD = D // H
F = 4 * D
G = 4
T = G * N
NB = B // G
P = 128
C = D // P
HC = H // C
FC = F // P
SCALE = 1.0 / math.sqrt(HD)
EPS = 1e-5
BIG = 1e30
X, Y = 0, 1

JOBS = [("T1", -1, C), ("WO1", -2, 2), ("QKV1", -1, 6), ("T2", -2, C), ("MLP1", -2, FC),
        ("WO0", 0, 2), ("QKV0", 1, 6), ("MLP2", -2, 2)]
BANKS = 3
FIRST_FULL, LAST_FULL = 3, NB - 2


def exists(b):
    return 0 <= b < NB if isinstance(b, int) else True


def positions():
    at, out = 0, {}
    for name, off, n in JOBS:
        out[name] = at
        at += n
    return out


POS = positions()
ALL_JOBS = [off for _, off, n in JOBS for _ in range(n)]
PER_BANK = len(ALL_JOBS) // BANKS
assert len(ALL_JOBS) % BANKS == 0


def uses_before(i, pos):
    def count(it):
        same = range(pos % BANKS, len(ALL_JOBS), BANKS)
        n = sum(exists(k + ALL_JOBS[q]) for k in range(-1, it) for q in same)
        return n + sum(exists(it + ALL_JOBS[q]) for q in same if q < pos)
    if isinstance(i, int):
        return count(i)
    return i * PER_BANK + (count(FIRST_FULL) - FIRST_FULL * PER_BANK)


def runs(i, phase):
    return exists(i if phase == X else i - 1)


def slot(i, phase, g):
    if isinstance(i, int):
        if phase == X:
            return g if i == 0 else 8 * i - G + g
        return 8 * i + g if i < NB else 8 * i - G + g
    return i * 8 + (g - G if phase == X else g)


def program(nc, x, xT, adj, w):
    ctx = ExitStack()
    with ctx:
        def sb(name, shape, dt=F32):
            return ctx.enter_context(nc.sbuf_tensor(name, shape, dt))

        def bank(name):
            return ctx.enter_context(nc.psum_tensor(name, [P, 512], F32))

        def sem(name):
            return ctx.enter_context(nc.semaphore(name))

        wqkv = [[sb(f"wqkv{l}{p}", [P, C, 3 * D], F32R) for p in "hl"] for l in (0, 1)]
        wo = [[sb(f"wo{l}{p}", [P, C, D], F32R) for p in "hl"] for l in (0, 1)]
        w1 = [sb(f"w1{p}", [P, C, F], F32R) for p in "hl"]
        w2 = [sb(f"w2{p}", [P, FC, D], F32R) for p in "hl"]
        ident = sb("ident", [P, P])
        par = sb("par", [P, 10 * C + FC])
        cols = par[:, 0:8 * C].rearrange("p (n c) -> p n c", c=C)
        lnp = par[:, 8 * C:10 * C].rearrange("p (n c) -> p n c", c=C)
        b1raw = par[:, 10 * C:]
        nbq = sb("nbq", [P, 2, C])
        bk = sb("bk", [P, 2, C])
        bv = sb("bv", [P, 2, C])
        b1 = sb("b1", [P, FC])
        gamma = sb("gamma", [P, D])
        beta = sb("beta", [P, D])
        bo = [sb(f"bo{l}", [P, D]) for l in (0, 1)]
        b2 = sb("b2", [P, D])
        ones = sb("ones", [P, P])
        bvw = sb("bvw", [P, 2, C, P])
        power = sb("power", [P, G])
        xy = sb("xy", [P, G, D])
        xTr = sb("xTr", [P, C, T])
        act = [sb(f"act{p}", [P, C, T], F32R) for p in "hl"]
        q = [sb(f"q{l}", [P, C, T]) for l in (0, 1)]
        kp = [sb(f"kp{l}", [P, C, HC, T]) for l in (0, 1)]
        v = [sb(f"v{l}", [P, G, D]) for l in (0, 1)]
        ot = [sb(f"ot{p}", [P, C, T], F32R) for p in "hl"]
        y0 = sb("y0", [P, G, D])
        r1 = sb("r1", [P, G, D])
        x1 = sb("x1", [P, G, D])
        xh2 = sb("xh2", [P, G, D])
        hf = sb("hf", [P, 2, T])
        hh = [sb(f"h{p}", [P, FC, T], F32R) for p in "hl"]
        m0 = sb("m0", [P, G, N])
        a1 = sb("a1", [P, G, N])
        m1 = sb("m1", [P, G, N])
        pm = sb("pm", [P, 2, H, N])
        pt = sb("pt", [P, 2, H, N])
        nmax = sb("nmax", [P, 2, H])
        rsum = sb("rsum", [P, 2, H])
        rinv = sb("rinv", [P, 2, H])
        stats = sb("stats", [P, 3, G, 6])
        mv = sb("mv", [P, 3, G, 2])
        veps = sb("veps", [P, 3, G])
        rstd = sb("rstd", [P, 3, G])

        ps_s = [bank("ps_s0"), bank("ps_s1")]
        ps_t = [bank("ps_t0"), bank("ps_t1")]
        ps_o = bank("ps_o")
        ps_j = [bank(f"ps_j{n}") for n in range(BANKS)]

        raw_loaded, par_loaded = sem("raw_loaded"), sem("par_loaded")
        x_loaded, xT_loaded, adj0_loaded, adj1_loaded = (
            sem("x_loaded"), sem("xT_loaded"), sem("adj0_loaded"), sem("adj1_loaded"))
        out_stored = sem("out_stored")
        ident_done, prep_split, prep_pe, prep_step, prep_act, prep_zero = (
            sem("ident_done"), sem("prep_split"), sem("prep_pe"), sem("prep_step"),
            sem("prep_act"), sem("prep_zero"))
        job_full = [sem(f"job_full{n}") for n in range(BANKS)]
        job_free = [sem(f"job_free{n}") for n in range(BANKS)]
        scores_full, masked, exp_done, rinv_done, norm_done = (
            sem("scores_full"), sem("masked"), sem("exp_done"), sem("rinv_done"), sem("norm_done"))
        pt_full, pt_a, pt_b, pv_done, ot_hi, ot_lo = (
            sem("pt_full"), sem("pt_a"), sem("pt_b"), sem("pv_done"), sem("ot_hi"), sem("ot_lo"))
        act_hi = [sem(f"act_hi{n}") for n in range(3)]
        act_lo0 = sem("act_lo0")
        mask0_done, mask1_done, mask1_step = sem("mask0_done"), sem("mask1_done"), sem("mask1_step")
        xb_done = sem("xb_done")
        y0_mul, y0_done, r1_done, x1b_done = (
            sem("y0_mul"), sem("y0_done"), sem("r1_done"), sem("x1b_done"))
        stats_done = [sem(f"stats_done{n}") for n in range(3)]
        aggr_done = [sem(f"aggr_done{n}") for n in range(3)]
        veps_done = [sem(f"veps_done{n}") for n in range(3)]
        rstd_done = [sem(f"rstd_done{n}") for n in range(3)]
        xhat_done = [sem(f"xhat_done{n}") for n in range(3)]
        h_hi, h_lo = sem("h_hi"), sem("h_lo")
        tick, carried = sem("tick"), sem("carried")

        def need(eng, s, n):
            if not isinstance(n, int) or n > 0:
                eng.wait_ge(s, n)

        def filled(eng, i, pos):
            eng.wait_ge(job_full[pos % BANKS], uses_before(i, pos) + 1)
            return ps_j[pos % BANKS]

        def taken(eng, i, *places):
            for pos in places:
                eng.wait_ge(job_free[pos % BANKS], uses_before(i, pos) + 1)

        def iterate(eng, body):
            for i in range(-1, FIRST_FULL):
                body(i)
            with eng.Fori(FIRST_FULL, LAST_FULL + 1) as i:
                body(i)
            for i in range(LAST_FULL + 1, NB + 3):
                body(i)

        def act_read(eng, i):
            for off, at, pos in ((-2, i, POS["MLP1"] + FC - 1), (-1, i, POS["QKV1"] + 5), (0, i - 1, POS["QKV0"] + 5)):
                if exists(i + off):
                    filled(eng, at, pos)
                    return

        raw0 = kp[0][:, :, :, :].rearrange("p c h t -> p (c h t)")
        raw1 = kp[1][:, :, :, :].rearrange("p c h t -> p (c h t)")
        raw_qkv = [raw0[:, l * 6 * D:(l + 1) * 6 * D].rearrange("p (c n) -> p c n", c=C) for l in (0, 1)]
        raw_o = [raw0[:, (12 + 2 * l) * D:(14 + 2 * l) * D].rearrange("p (c n) -> p c n", c=C)
                 for l in (0, 1)]
        raw_1 = raw1[:, 0:C * F].rearrange("p (c n) -> p c n", c=C)
        raw_2 = raw1[:, C * F:C * F + FC * D].rearrange("p (c n) -> p c n", c=FC)
        BQ, BK, BV, LG, LB = 0, 2, 4, 6, 7

        block = ctx.enter_context(nc.Block())

        @block.sync
        def _(sp):
            x_b = x.rearrange("(b g) t f -> b t g f", g=G)
            a_b = adj.rearrange("(b g) q k -> b q g k", g=G)
            o_b = w["out"].rearrange("(b g) t f -> b t g f", g=G)
            xT_v = xT.rearrange("(c p) n -> p c n", p=P)

            def row(name):
                return w[name].rearrange("(a n) -> a n", a=1).to_broadcast([P, D])

            for l in (0, 1):
                for n, part in enumerate(("q", "k", "v")):
                    sp.dma_start(raw_qkv[l][:, :, n * D:(n + 1) * D],
                                 w[f"w{part}{l}"].rearrange("(c p) n -> p c n", p=P)).then_inc(raw_loaded, 16)
            for l in (0, 1):
                sp.dma_start(raw_o[l], w[f"wo{l}"].rearrange("(c p) n -> p c n", p=P)).then_inc(raw_loaded, 16)
            sp.dma_start(raw_1, w["w1"].rearrange("(c p) n -> p c n", p=P)).then_inc(raw_loaded, 16)
            sp.dma_start(raw_2, w["w2"].rearrange("(c p) n -> p c n", p=P)).then_inc(raw_loaded, 16)
            sp.dma_start(par[:, :], w["columns"]).then_inc(par_loaded, 16)
            for dst, name in ((gamma, "gamma"), (beta, "beta"), (bo[0], "bo0"), (bo[1], "bo1"), (b2, "b2")):
                sp.dma_start(dst[:, :], row(name)).then_inc(par_loaded, 16)

            def body(i):
                if exists(i + 1):
                    need(sp, act_hi[0], 2 * (i + 1))
                    need(sp, act_lo0, 2 * (i + 1))
                    sp.dma_start(xTr[:, :, :], xT_v[:, :, bass.ts(i + 1, T)]).then_inc(xT_loaded, 16)
                if exists(i - 3):
                    taken(sp, i - 1, POS["MLP2"], POS["MLP2"] + 1)
                    sp.dma_start(o_b[bass.ds(i - 3, 1), :, :, :].rearrange("a t g f -> t (a g) f"),
                                 x1[:, :, :]).then_inc(out_stored, 16)
                if exists(i):
                    if exists(i - 1):
                        filled(sp, i, POS["T1"] + C - 1)
                    sp.dma_start(xy[:, :, :], x_b[bass.ds(i, 1), :, :, :].rearrange("a t g f -> t (a g) f")) \
                      .then_inc(x_loaded, 16)
                if exists(i):
                    need(sp, mask1_done, i)
                    sp.dma_start(a1[:, :, :].bitcast(I32),
                                 a_b[bass.ds(i, 1), :, :, :].rearrange("a q g k -> q (a g) k")) \
                      .then_inc(adj1_loaded, 16)
                if exists(i + 1):
                    if exists(i):
                        need(sp, masked, 2 * slot(i, X, G - 1) + 2)
                    sp.dma_start(m0[:, :, :].bitcast(I32),
                                 a_b[bass.ds(i + 1, 1), :, :, :].rearrange("a q g k -> q (a g) k")) \
                      .then_inc(adj0_loaded, 16)

            iterate(sp, body)
            sp.wait_ge(out_stored, 16 * NB)

        @block.tensor
        def _(pe):
            mm = nc.tensor.matmul

            pe.wait_ge(raw_loaded, 16 * 10)
            pe.wait_ge(par_loaded, 16 * 6)
            for n in range(3 * C):
                for c in range(C):
                    last = mm(ps_j[0][:, n:n + 1], raw_qkv[1][:, c, n * P:(n + 1) * P],
                              cols[:, LB, c:c + 1], start=(c == 0), stop=(c == C - 1))
            for m in range(FC):
                for c in range(C):
                    last = mm(ps_j[0][:, 3 * C + m:3 * C + m + 1], raw_1[:, c, m * P:(m + 1) * P],
                              lnp[:, 1, c:c + 1], start=(c == 0), stop=(c == C - 1))
            last.then_inc(prep_pe, 1)
            pe.wait_ge(prep_step, 3)
            for l in (0, 1):
                for c in range(C):
                    last = mm(ps_j[1 + l][:, 0:D], bvw[:, l, c, :], raw_o[l][:, c, :],
                              start=(c == 0), stop=(c == C - 1))
            last.then_inc(prep_pe, 1)
            pe.wait_ge(prep_split, 1)
            pe.wait_ge(prep_act, 2)
            pe.wait_ge(ident_done, 3)

            def open_job(i, pos):
                need(pe, job_free[pos % BANKS], uses_before(i, pos))
                return ps_j[pos % BANKS]

            def scores(i, phase, g, c):
                if runs(i, phase):
                    l, n = phase, slot(i, phase, g)
                    if g == 0 and c == 0:
                        taken(pe, i - 1 if phase == X else i, *(POS[f"QKV{l}"] + m for m in range(1, 4)))
                    need(pe, masked, 2 * n - C + c + 1)
                    mm(ps_s[c][:, :].rearrange("p (h k) -> p h k", h=HC), q[l][:, c, g * N:(g + 1) * N],
                       kp[l][:, c, :, g * N:(g + 1) * N], start=True, stop=True).then_inc(scores_full, 1)

            def flip(i, phase, g, c):
                if runs(i, phase):
                    n = slot(i, phase, g)
                    need(pe, norm_done, 2 * n + c + 1)
                    need(pe, (pt_a, pt_b)[c], n)
                    for j in range(HC):
                        last = nc.tensor.transpose(ps_t[c][:, j * N:(j + 1) * N],
                                                   pm[:, g % 2, c * HC + j, :], ident[:, :])
                    last.then_inc(pt_full, 1)

            def values(i, phase, g):
                if runs(i, phase):
                    l, n = phase, slot(i, phase, g)
                    if g == 0:
                        taken(pe, i - 1 if phase == X else i, POS[f"QKV{l}"] + 4, POS[f"QKV{l}"] + 5)
                    need(pe, pt_a, n + 1)
                    need(pe, pt_b, n + 1)
                    need(pe, ot_lo, n)
                    for h in range(H):
                        j = h % HC
                        last = mm(ps_o[j * HD:(j + 1) * HD, (h // HC) * N:(h // HC + 1) * N],
                                  v[l][:, g, h * HD:(h + 1) * HD], pt[:, g % 2, h, :], start=True, stop=True)
                    last.then_inc(pv_done, 1)

            def split_mm(out, parts, wparts, pick, wpick, chunks):
                terms = [(c, a, b) for c in range(chunks) for a, b in ((0, 0), (0, 1), (1, 0))]
                for n, (c, a, b) in enumerate(terms):
                    last = mm(out, pick(parts[a], c), wpick(wparts[b], c),
                              start=(n == 0), stop=(n == len(terms) - 1))
                return last

            def flip_rows(i, name, c):
                off, src, k = {"T1": (-1, xy, 1), "T2": (-2, xh2, 2)}[name]
                if exists(i + off):
                    pos = POS[name] + c
                    need(pe, xhat_done[k], i + off + 1)
                    out = open_job(i, pos)
                    for g in range(G):
                        last = nc.tensor.transpose(out[:, g * N:(g + 1) * N],
                                                   src[:, g, c * P:(c + 1) * P], ident[:, :])
                    last.then_inc(job_full[pos % BANKS], 1)

            def out_proj(i, l, j):
                off = 0 if l == 0 else -2
                if not exists(i + off):
                    return
                pos = POS[f"WO{l}"] + j
                n = slot(i, X, 2 * j + 1) if l == 0 else slot(i - 1, Y, 2 * j + 1)
                need(pe, ot_lo, n + 1)
                out = open_job(i, pos)
                for g in (2 * j, 2 * j + 1):
                    last = split_mm(out[:, (g % 2) * D:(g % 2 + 1) * D], ot, wo[l],
                                    lambda t, c: t[:, c, g * N:(g + 1) * N], lambda t, c: t[:, c, :], C)
                last.then_inc(job_full[pos % BANKS], 1)

            def qkv(i, l, n):
                b = i + (1 if l == 0 else -1)
                if exists(b):
                    pos = POS[f"QKV{l}"] + n
                    if n == 0 and l == 0:
                        need(pe, act_hi[0], C * (b + 1))
                        need(pe, act_lo0, C * (b + 1))
                    elif n == 0:
                        taken(pe, i, POS["T1"], POS["T1"] + 1)
                    out = open_job(i, pos)
                    if n < 4:
                        last = split_mm(out[:, :], wqkv[l], act,
                                        lambda t, c: t[:, c, n * P:(n + 1) * P], lambda t, c: t[:, c, :], C)
                    else:
                        for g in (2 * (n - 4), 2 * (n - 4) + 1):
                            last = split_mm(out[:, (g % 2) * D:(g % 2 + 1) * D], act, wqkv[l],
                                            lambda t, c: t[:, c, g * N:(g + 1) * N],
                                            lambda t, c: t[:, c, 2 * D:3 * D], C)
                    last.then_inc(job_full[pos % BANKS], 1)

            def mlp_up(i, m):
                b = i - 2
                if not exists(b):
                    return
                pos = POS["MLP1"] + m
                if m == 0:
                    taken(pe, i, POS["T2"], POS["T2"] + 1)
                out = open_job(i, pos)
                split_mm(out[:, :], w1, act, lambda t, c: t[:, c, m * P:(m + 1) * P],
                         lambda t, c: t[:, c, :], C).then_inc(job_full[pos % BANKS], 1)

            def mlp_down(i, g):
                b = i - 2
                if not exists(b):
                    return
                pos = POS["MLP2"] + g // 2
                out = ps_j[pos % BANKS]
                if g % 2 == 0:
                    need(pe, h_lo, FC * (b + 1))
                    open_job(i, pos)
                last = split_mm(out[:, (g % 2) * D:(g % 2 + 1) * D], hh, w2,
                                lambda t, c: t[:, c, g * N:(g + 1) * N], lambda t, c: t[:, c, :], FC)
                if g % 2 == 1:
                    last.then_inc(job_full[pos % BANKS], 1)

            def body(i):
                values(i - 1, Y, 0); flip(i - 1, Y, 2, 0); scores(i, X, 0, 0); flip(i - 1, Y, 2, 1)
                values(i - 1, Y, 1); scores(i, X, 0, 1); flip_rows(i, "T1", 0); flip(i - 1, Y, 3, 0)
                scores(i, X, 1, 0); flip(i - 1, Y, 3, 1); values(i - 1, Y, 2); flip_rows(i, "T1", 1)
                scores(i, X, 1, 1); out_proj(i, 1, 0); values(i - 1, Y, 3); flip(i, X, 0, 0)
                scores(i, X, 2, 0); flip(i, X, 0, 1); scores(i, X, 2, 1); out_proj(i, 1, 1); qkv(i, 1, 0)
                qkv(i, 1, 1); qkv(i, 1, 2); values(i, X, 0); qkv(i, 1, 3); flip(i, X, 1, 0); qkv(i, 1, 4)
                flip(i, X, 1, 1); scores(i, X, 3, 0); qkv(i, 1, 5); flip_rows(i, "T2", 0)
                flip_rows(i, "T2", 1); scores(i, X, 3, 1); flip(i, X, 2, 0); scores(i, Y, 0, 0)
                values(i, X, 1); flip(i, X, 2, 1); scores(i, Y, 0, 1); mlp_up(i, 0); mlp_up(i, 1)
                mlp_up(i, 2); flip(i, X, 3, 0); flip(i, X, 3, 1); values(i, X, 2); mlp_up(i, 3); mlp_up(i, 4)
                mlp_up(i, 5); mlp_up(i, 6); mlp_up(i, 7); values(i, X, 3); out_proj(i, 0, 0)
                scores(i, Y, 1, 0); scores(i, Y, 1, 1); out_proj(i, 0, 1); qkv(i, 0, 0); qkv(i, 0, 1)
                qkv(i, 0, 2); qkv(i, 0, 3); flip(i, Y, 0, 0); scores(i, Y, 2, 0); flip(i, Y, 0, 1)
                scores(i, Y, 2, 1); qkv(i, 0, 4); flip(i, Y, 1, 0); scores(i, Y, 3, 0); flip(i, Y, 1, 1)
                mlp_down(i, 0); qkv(i, 0, 5); scores(i, Y, 3, 1); mlp_down(i, 1); mlp_down(i, 2)
                mlp_down(i, 3)

            iterate(pe, body)

        @block.scalar
        def _(sc):
            sc.wait_ge(prep_step, 2)
            nc.scalar.activation(nbq[:, :, :], cols[:, BQ:BQ + 2, :], ACT.Copy, scale=-SCALE).then_inc(prep_act, 1)
            nc.scalar.activation(bk[:, :, :], cols[:, BK:BK + 2, :], ACT.Copy).then_inc(prep_act, 1)
            sc.wait_ge(prep_act, 2)
            sc.wait_ge(prep_zero, 2)

            def exp(i, phase, g, c):
                if runs(i, phase):
                    need(sc, masked, 2 * slot(i, phase, g) + c + 1)
                    for h in range(c * HC, (c + 1) * HC):
                        last = nc.scalar.activation(pm[:, g % 2, h, :], pm[:, g % 2, h, :], ACT.Exp,
                                                    bias=nmax[:, g % 2, h:h + 1], scale=-1.0,
                                                    accum_out=rsum[:, g % 2, h:h + 1])
                    last.then_inc(exp_done, 1)

            def copy_pt(i, phase, g):
                if runs(i, phase):
                    need(sc, pt_full, 2 * slot(i, phase, g) + 1)
                    nc.scalar.activation(pt[:, g % 2, 0:HC, :], ps_t[0][:, :].rearrange("p (h q) -> p h q", h=HC),
                                         ACT.Copy).then_inc(pt_a, 1)

            def out_hi(i, phase, g):
                if runs(i, phase):
                    need(sc, pv_done, slot(i, phase, g) + 1)
                    nc.scalar.activation(ot[0][:, :, g * N:(g + 1) * N],
                                         ps_o[:, 0:C * N].rearrange("p (c q) -> p c q", c=C),
                                         ACT.Copy).then_inc(ot_hi, 1)

            def qk_out(i, l, n):
                if exists(i + (1 if l == 0 else -1)):
                    pos = POS[f"QKV{l}"] + n
                    src = filled(sc, i, pos)
                    c = n % C
                    if n < 2:
                        last = nc.scalar.activation(q[l][:, c, :], src[:, :], ACT.Identity,
                                                    bias=nbq[:, l, c:c + 1], scale=-SCALE)
                    else:
                        for j in range(HC):
                            rows = slice(j * HD, (j + 1) * HD)
                            last = nc.scalar.activation(kp[l][rows, c, j, :], src[rows, :], ACT.Identity,
                                                        bias=bk[rows, l, c:c + 1])
                    last.then_inc(job_free[pos % BANKS], 1)

            def hi(i, name, c):
                off, k = {"T1": (-1, 1), "T2": (-2, 2)}[name]
                if exists(i + off):
                    src = filled(sc, i, POS[name] + c)
                    nc.scalar.activation(act[0][:, c, :], src[:, :], ACT.Copy).then_inc(act_hi[k], 1)

            def x_hi(i, c):
                if exists(i + 1):
                    if c == 0:
                        need(sc, xT_loaded, 16 * (i + 2))
                        act_read(sc, i)
                    nc.scalar.activation(act[0][:, c, :], xTr[:, c, :], ACT.Copy).then_inc(act_hi[0], 1)

            def gelu(i, m):
                b = i - 2
                if exists(b):
                    src = filled(sc, i, POS["MLP1"] + m)
                    need(sc, h_lo, FC * b + m - 1)
                    nc.scalar.activation(hf[:, m % 2, :], src[:, :], ACT.Gelu, bias=b1[:, m:m + 1])\
                      .then_inc(job_free[(POS["MLP1"] + m) % BANKS], 1)

            def body(i):
                exp(i - 1, Y, 3, 0); exp(i - 1, Y, 3, 1); out_hi(i - 1, Y, 0); copy_pt(i - 1, Y, 2)
                out_hi(i - 1, Y, 1); exp(i, X, 0, 0); exp(i, X, 0, 1); hi(i, "T1", 0); out_hi(i - 1, Y, 2)
                copy_pt(i - 1, Y, 3); hi(i, "T1", 1); exp(i, X, 1, 0); out_hi(i - 1, Y, 3); copy_pt(i, X, 0)
                exp(i, X, 1, 1); exp(i, X, 2, 0); exp(i, X, 2, 1); qk_out(i, 1, 0); qk_out(i, 1, 1)
                qk_out(i, 1, 2); qk_out(i, 1, 3); copy_pt(i, X, 1); out_hi(i, X, 0); hi(i, "T2", 0)
                hi(i, "T2", 1); exp(i, X, 3, 0); exp(i, X, 3, 1); out_hi(i, X, 1); copy_pt(i, X, 2)
                exp(i, Y, 0, 0); gelu(i, 0); copy_pt(i, X, 3); gelu(i, 1); gelu(i, 2); gelu(i, 3); gelu(i, 4)
                out_hi(i, X, 2); gelu(i, 5); x_hi(i, 0); x_hi(i, 1); out_hi(i, X, 3); gelu(i, 6); gelu(i, 7)
                exp(i, Y, 0, 1); exp(i, Y, 1, 0); qk_out(i, 0, 0); exp(i, Y, 1, 1); qk_out(i, 0, 1)
                copy_pt(i, Y, 0); qk_out(i, 0, 3); qk_out(i, 0, 2); exp(i, Y, 2, 0); copy_pt(i, Y, 1)
                exp(i, Y, 2, 1)

            iterate(sc, body)

        @block.vector
        def _(dve):
            tt, ts = nc.vector.tensor_tensor, nc.vector.tensor_scalar

            dve.wait_ge(raw_loaded, 16 * 10)
            dve.wait_ge(par_loaded, 16 * 6)
            nc.vector.memset(ones[:, :], 1.0)
            nc.vector.memset(power[:, :], -0.5)
            parts = []
            for c in range(C):
                parts += [(wqkv[0][0][:, c, :], wqkv[0][1][:, c, :], raw_qkv[0][:, c, :], 1.0),
                          (wqkv[1][0][:, c, :], wqkv[1][1][:, c, :], raw_qkv[1][:, c, :], cols[:, LG, c:c + 1]),
                          (w1[0][:, c, :], w1[1][:, c, :], raw_1[:, c, :], lnp[:, 0, c:c + 1])]
            for l in (0, 1):
                parts.append((wo[l][0][:, :, :], wo[l][1][:, :, :], raw_o[l], 1.0))
            for k in range(2):
                half = slice(k * FC // 2, (k + 1) * FC // 2)
                parts.append((w2[0][:, half, :], w2[1][:, half, :], raw_2[:, half, :], 1.0))
            for k, (h, _, raw, by) in enumerate(parts):
                ts(h, raw, by, None, ALU.mult).then_inc(tick, 1)
            dve.wait_ge(tick, len(parts))
            for k, (h, lo, raw, by) in enumerate(parts):
                nc.vector.scalar_tensor_tensor(lo, raw, by, h.bitcast(F32), ALU.mult, ALU.subtract)\
                  .then_inc(tick, 1)
            dve.wait_ge(prep_pe, 1)
            shifts = ps_j[0][:, 0:3 * C + FC]
            for n, to in ((0, BQ + 1), (1, BK + 1), (2, BV + 1)):
                last = tt(cols[:, to, :], cols[:, to, :], shifts[:, n * C:(n + 1) * C], ALU.add)
            last.then_inc(prep_step, 1)
            tt(b1[:, :], b1raw, shifts[:, 3 * C:], ALU.add).then_inc(prep_step, 1)
            dve.wait_ge(prep_step, 2)
            for l in (0, 1):
                for c in range(C):
                    last = ts(bvw[:, l, c, :], ones[:, :], cols[:, BV + l, c:c + 1], None, ALU.mult)
            last.then_inc(prep_step, 1)
            dve.wait_ge(prep_pe, 2)
            for l in (0, 1):
                last = tt(bo[l][:, :], bo[l][:, :], ps_j[1 + l][:, 0:D], ALU.add)
            last.then_inc(prep_step, 1)
            dve.wait_ge(tick, 2 * len(parts))
            for l in (0, 1):
                nc.vector.memset(kp[l][:, :, :, :], 0.0).then_inc(prep_zero, 1)
            dve.wait_ge(prep_zero, 2)
            dve.sem_inc(prep_split, 1)

            def mask0(i):
                b = i + 1
                if exists(b):
                    dve.wait_ge(adj0_loaded, 16 * (b + 1))
                    ts(m0[:, :, :], m0[:, :, :].bitcast(I32), 0, BIG, ALU.is_equal, ALU.mult)\
                      .then_inc(mask0_done, 1)

            def mask1(i):
                b = i - 1
                if exists(b):
                    dve.wait_ge(adj1_loaded, 16 * (b + 1))
                    a = a1[:, :, :].bitcast(I32)
                    nc.vector.scalar_tensor_tensor(m1[:, :, :], a, -0.1, a, ALU.mult, ALU.mult)\
                      .then_inc(mask1_step, 1)
                    dve.wait_ge(mask1_step, 2 * b + 1)
                    ts(a1[:, :, :], a, 0, BIG, ALU.is_le, ALU.mult).then_inc(mask1_step, 1)
                    dve.wait_ge(mask1_step, 2 * b + 2)
                    tt(m1[:, :, :], m1[:, :, :], a1[:, :, :], ALU.add).then_inc(mask1_done, 1)

            def mask_scores(i, phase, g, c):
                if runs(i, phase):
                    if g == 0 and c == 0:
                        dve.wait_ge((mask0_done, mask1_done)[phase], (i if phase == X else i - 1) + 1)
                    m = (m0, m1)[phase]
                    dve.wait_ge(scores_full, 2 * slot(i, phase, g) + c + 1)
                    dve.sem_inc(carried, 1)
                    for j in range(HC):
                        h = c * HC + j
                        last = nc.vector.tensor_tensor_reduce(
                            out=pm[:, g % 2, h, :], in0=ps_s[c][:, j * N:(j + 1) * N],
                            in1=m[:, g, :], scale=1.0, scalar=3e38, op0=ALU.add, op1=ALU.min,
                            accum_out=nmax[:, g % 2, h:h + 1])
                    last.then_inc(masked, 1)

            def recip(i, phase, g):
                if runs(i, phase):
                    dve.wait_ge(exp_done, 2 * slot(i, phase, g) + 2)
                    nc.vector.reciprocal(rinv[:, g % 2, :], rsum[:, g % 2, :]).then_inc(rinv_done, 1)

            def copy_pt(i, phase, g):
                if runs(i, phase):
                    dve.wait_ge(pt_full, 2 * slot(i, phase, g) + 2)
                    nc.vector.tensor_copy(pt[:, g % 2, HC:H, :], ps_t[1][:, :].rearrange("p (h q) -> p h q", h=HC))\
                      .then_inc(pt_b, 1)

            def out_lo(i, phase, g):
                if runs(i, phase):
                    dve.wait_ge(ot_hi, slot(i, phase, g) + 1)
                    cols_g = slice(g * N, (g + 1) * N)
                    tt(ot[1][:, :, cols_g], ps_o[:, 0:C * N].rearrange("p (c q) -> p c q", c=C),
                       ot[0][:, :, cols_g].bitcast(F32), ALU.subtract).then_inc(ot_lo, 1)

            def lo(i, name, c):
                off, k = {"T1": (-1, 1), "T2": (-2, 2)}[name]
                b = i + off
                if exists(b):
                    pos = POS[name] + c
                    filled(dve, i, pos)
                    dve.wait_ge(act_hi[k], C * b + c + 1)
                    tt(act[1][:, c, :], ps_j[pos % BANKS][:, :], act[0][:, c, :].bitcast(F32),
                       ALU.subtract).then_inc(job_free[pos % BANKS], 1)

            def x_lo(i, c):
                if exists(i + 1):
                    dve.wait_ge(act_hi[0], C * (i + 1) + c + 1)
                    tt(act[1][:, c, :], xTr[:, c, :], act[0][:, c, :].bitcast(F32), ALU.subtract)\
                      .then_inc(act_lo0, 1)

            def v_out(i, l, j):
                if exists(i + (1 if l == 0 else -1)):
                    pos = POS[f"QKV{l}"] + 4 + j
                    src = filled(dve, i, pos)
                    nc.vector.tensor_copy(v[l][:, 2 * j:2 * j + 2, :],
                                          src[:, :].rearrange("p (g n) -> p g n", g=2))\
                      .then_inc(job_free[pos % BANKS], 1)

            def residual(i, name, j):
                off, out, add = {"WO0": (0, xy, xy), "WO1": (-2, x1, r1), "MLP2": (-2, x1, x1)}[name]
                b = i + off
                if exists(b):
                    ready = {"WO0": xb_done, "WO1": r1_done, "MLP2": x1b_done}[name]
                    dve.wait_ge(ready, b + 1)
                    if name == "WO1":
                        need(dve, out_stored, 16 * b)
                    pos = POS[name] + j
                    src = filled(dve, i, pos)
                    gs = slice(2 * j, 2 * j + 2)
                    tt(out[:, gs, :], src[:, :].rearrange("p (g n) -> p g n", g=2), add[:, gs, :],
                       ALU.add).then_inc(job_free[pos % BANKS], 1)

            NORMS = ((xy, xy, 0), (y0, xy, 0), (x1, xh2, -2))

            def norm_stats(i, k):
                src, _, off = NORMS[k]
                b = i + off
                if exists(b):
                    if k == 1:
                        dve.wait_ge(y0_done, b + 1)
                    else:
                        name = ("WO0", None, "WO1")[k]
                        taken(dve, i, POS[name], POS[name] + 1)
                    for g in range(G):
                        last = nc.vector.bn_stats(stats[:, k, g, :], src[:, g, :])
                    last.then_inc(stats_done[k], 1)
                    dve.wait_ge(stats_done[k], b + 1)
                    dve.sem_inc(carried, 1)
                    for g in range(G):
                        last = nc.vector.bn_aggr(mv[:, k, g, :], stats[:, k, g, :])
                    last.then_inc(aggr_done[k], 1)
                    dve.wait_ge(aggr_done[k], b + 1)
                    ts(veps[:, k, :], mv[:, k, :, 1], EPS, None, ALU.add).then_inc(veps_done[k], 1)

            def norm_rows(i, k):
                src, out, off = NORMS[k]
                b = i + off
                if exists(b):
                    dve.wait_ge(rstd_done[k], b + 1)
                    for g in range(G):
                        last = ts(out[:, g, :], src[:, g, :], mv[:, k, g, 0:1], rstd[:, k, g:g + 1],
                                  ALU.subtract, ALU.mult)
                    last.then_inc(xhat_done[k], 1)

            def split_h(i, m):
                b = i - 2
                if exists(b):
                    taken(dve, i, POS["MLP1"] + m)
                    nc.vector.tensor_copy(hh[0][:, m, :], hf[:, m % 2, :]).then_inc(h_hi, 1)
                    dve.wait_ge(h_hi, FC * b + m + 1)
                    tt(hh[1][:, m, :], hf[:, m % 2, :], hh[0][:, m, :].bitcast(F32),
                       ALU.subtract).then_inc(h_lo, 1)

            def body(i):
                mask_scores(i - 1, Y, 3, 1); copy_pt(i - 1, Y, 1); norm_rows(i - 1, 1); recip(i - 1, Y, 3)
                out_lo(i - 1, Y, 0); mask_scores(i, X, 0, 0); copy_pt(i - 1, Y, 2); mask_scores(i, X, 0, 1)
                out_lo(i - 1, Y, 1); residual(i - 1, "MLP2", 1); mask_scores(i, X, 1, 0); copy_pt(i - 1, Y, 3)
                recip(i, X, 0); out_lo(i - 1, Y, 2); lo(i, "T1", 0); lo(i, "T1", 1); mask_scores(i, X, 1, 1)
                out_lo(i - 1, Y, 3); mask_scores(i, X, 2, 0); residual(i, "WO1", 0); mask_scores(i, X, 2, 1)
                residual(i, "WO1", 1); copy_pt(i, X, 0); recip(i, X, 1); norm_stats(i, 2); mask1(i)
                norm_rows(i, 2); recip(i, X, 2); v_out(i, 1, 0); mask_scores(i, X, 3, 0); v_out(i, 1, 1)
                copy_pt(i, X, 1); out_lo(i, X, 0); mask_scores(i, X, 3, 1); lo(i, "T2", 1); lo(i, "T2", 0)
                mask_scores(i, Y, 0, 0); recip(i, X, 3); mask_scores(i, Y, 0, 1); copy_pt(i, X, 2)
                out_lo(i, X, 1); split_h(i, 0); split_h(i, 1); split_h(i, 2); split_h(i, 3); copy_pt(i, X, 3)
                out_lo(i, X, 2); split_h(i, 4); split_h(i, 5); out_lo(i, X, 3); x_lo(i, 1); x_lo(i, 0)
                residual(i, "WO0", 0); mask_scores(i, Y, 1, 0); mask_scores(i, Y, 1, 1); residual(i, "WO0", 1)
                recip(i, Y, 0); norm_stats(i, 0); split_h(i, 6); recip(i, Y, 1); mask_scores(i, Y, 2, 0)
                split_h(i, 7); copy_pt(i, Y, 0); norm_rows(i, 0); mask_scores(i, Y, 2, 1); v_out(i, 0, 1)
                v_out(i, 0, 0); mask_scores(i, Y, 3, 0); mask0(i); recip(i, Y, 2); norm_stats(i, 1)
                residual(i, "MLP2", 0)

            iterate(dve, body)

        @block.gpsimd
        def _(pool):
            tt = nc.gpsimd.tensor_tensor
            nc.gpsimd.memset(ident[:, :], 0.0).then_inc(ident_done, 1)
            pool.wait_ge(ident_done, 1)
            nc.gpsimd.affine_select(out=ident[:, :], in_=ident[:, :], compare_op=ALU.not_equal, fill=1.0,
                                    base=0, pattern=[[-1, P]], channel_multiplier=1).then_inc(ident_done, 2)
            pool.wait_ge(prep_step, 4)

            def over_rows(t):
                return t[:, :].rearrange("p (a n) -> p a n", a=1).to_broadcast([P, G, D])

            def normalise(i, phase, g, c):
                if runs(i, phase):
                    pool.wait_ge(rinv_done, slot(i, phase, g) + 1)
                    hs = slice(c * HC, (c + 1) * HC)
                    tt(pm[:, g % 2, hs, :], pm[:, g % 2, hs, :],
                       rinv[:, g % 2, hs].rearrange("p (h a) -> p h a", a=1).to_broadcast([P, HC, N]),
                       ALU.mult).then_inc(norm_done, 1)

            def root(i, k):
                b = i + (0, 0, -2)[k]
                if exists(b):
                    pool.wait_ge(veps_done[k], b + 1)
                    tt(rstd[:, k, :], veps[:, k, :], power[:, :], ALU.pow).then_inc(rstd_done[k], 1)

            def add_bo1(i):
                if exists(i - 1):
                    if exists(i - 2):
                        taken(pool, i, POS["WO1"], POS["WO1"] + 1)
                    pool.wait_ge(y0_done, i)
                    tt(r1[:, :, :], y0[:, :, :], over_rows(bo[1]), ALU.add).then_inc(r1_done, 1)

            def add_b2(i):
                if exists(i - 2):
                    pool.wait_ge(xhat_done[2], i - 1)
                    tt(x1[:, :, :], x1[:, :, :], over_rows(b2), ALU.add).then_inc(x1b_done, 1)

            def add_bo0(i):
                if exists(i):
                    pool.wait_ge(x_loaded, 16 * (i + 1))
                    tt(xy[:, :, :], xy[:, :, :], over_rows(bo[0]), ALU.add).then_inc(xb_done, 1)

            def scale_y0(i):
                if exists(i):
                    pool.wait_ge(xhat_done[0], i + 1)
                    tt(y0[:, :, :], xy[:, :, :], over_rows(gamma), ALU.mult).then_inc(y0_mul, 1)

            def shift_y0(i):
                if exists(i):
                    pool.wait_ge(y0_mul, i + 1)
                    tt(y0[:, :, :], y0[:, :, :], over_rows(beta), ALU.add).then_inc(y0_done, 1)

            def body(i):
                normalise(i - 1, Y, 2, 0); normalise(i - 1, Y, 2, 1); root(i - 1, 1)
                normalise(i - 1, Y, 3, 0); normalise(i - 1, Y, 3, 1); normalise(i, X, 0, 0)
                normalise(i, X, 0, 1); normalise(i, X, 1, 0); normalise(i, X, 1, 1); root(i, 2); add_bo1(i)
                normalise(i, X, 2, 0); normalise(i, X, 2, 1); normalise(i, X, 3, 0); normalise(i, X, 3, 1)
                add_bo0(i); normalise(i, Y, 0, 0); normalise(i, Y, 0, 1); root(i, 0); normalise(i, Y, 1, 0)
                normalise(i, Y, 1, 1); scale_y0(i); shift_y0(i); add_b2(i)

            iterate(pool, body)


WEIGHTS = {
    "wq0": "L0_gnn_Wq", "bq0": "L0_gnn_bq", "wk0": "L0_gnn_Wk", "bk0": "L0_gnn_bk",
    "wv0": "L0_gnn_Wv", "bv0": "L0_gnn_bv", "wo0": "L0_gnn_Wo", "bo0": "L0_gnn_bo",
    "gamma": "L0_gnn_gamma", "beta": "L0_gnn_beta",
    "ln1_g": "L1_gnn_ln1_g", "ln1_b": "L1_gnn_ln1_b", "ln2_g": "L1_gnn_ln2_g", "ln2_b": "L1_gnn_ln2_b",
    "wq1": "L1_gnn_wq", "bq1": "L1_gnn_bq", "wk1": "L1_gnn_wk", "bk1": "L1_gnn_bk",
    "wv1": "L1_gnn_wv", "bv1": "L1_gnn_bv", "wo1": "L1_gnn_wo", "bo1": "L1_gnn_bo",
    "w1": "L1_gnn_w1", "b1": "L1_gnn_b1", "w2": "L1_gnn_w2", "b2": "L1_gnn_b2",
}

COLUMNS = ("bq0", "bq1", "bk0", "bk1", "bv0", "bv1", "ln1_g", "ln1_b", "ln2_g", "ln2_b", "b1")


def kernel(**inputs):
    import concourse.bacc as _bacc
    from concourse.bass_utils import run_bass_kernel_spmd as _run

    nc = _bacc.Bacc("TRN2", target_bir_lowering=False, num_devices=1, dynamic_dma_scratch_size=1024)
    x = np.ascontiguousarray(inputs["x"])
    arrays = {"x": x, "xT": np.ascontiguousarray(x.reshape(B * N, D).T),
              "adj": np.ascontiguousarray(inputs["adj"])}
    for short, name in WEIGHTS.items():
        if short not in COLUMNS:
            arrays[short] = np.ascontiguousarray(inputs[name])
    arrays["columns"] = np.ascontiguousarray(
        np.concatenate([inputs[WEIGHTS[short]].reshape(-1, P).T for short in COLUMNS], axis=1))
    arrays = {f"in_{k}": a for k, a in arrays.items()}
    aps = {k[3:]: nc.dram_tensor(k, a.shape, mybir.dt.from_np(a.dtype), kind="ExternalInput").ap()
           for k, a in arrays.items()}
    aps["out"] = nc.dram_tensor("out", (B, N, D), F32, kind="ExternalOutput").ap()
    program(nc, aps.pop("x"), aps.pop("xT"), aps.pop("adj"), aps)
    r = _run(nc, [arrays], core_ids=[0])
    return r.results[0]["out"]
```

```python
import math
from contextlib import ExitStack

import numpy as np

import concourse.bass as bass
from concourse import mybir

F32 = mybir.dt.float32
F32R = mybir.dt.float32r
I32 = mybir.dt.int32
ALU = mybir.AluOpType
ACT = mybir.ActivationFunctionType

B, N, D, H = 128, 128, 256, 8
HD = D // H
F = 4 * D
G = 4
T = G * N
NB = B // G
P = 128
C = D // P
HC = H // C
FC = F // P
SCALE = 1.0 / math.sqrt(HD)
EPS = 1e-5
BIG = 1e30
X, Y = 0, 1

JOBS = [("T1", -1, C), ("WO1", -2, 2), ("QKV1", -1, 6), ("T2", -2, C), ("MLP1", -2, FC),
        ("WO0", 0, 2), ("QKV0", 1, 6), ("MLP2", -2, 2)]
BANKS = 3
FIRST_FULL, LAST_FULL = 3, NB - 2


def exists(b):
    return 0 <= b < NB if isinstance(b, int) else True


def positions():
    at, out = 0, {}
    for name, off, n in JOBS:
        out[name] = at
        at += n
    return out


POS = positions()
ALL_JOBS = [off for _, off, n in JOBS for _ in range(n)]
PER_BANK = len(ALL_JOBS) // BANKS
assert len(ALL_JOBS) % BANKS == 0


def uses_before(i, pos):
    def count(it):
        same = range(pos % BANKS, len(ALL_JOBS), BANKS)
        n = sum(exists(k + ALL_JOBS[q]) for k in range(-1, it) for q in same)
        return n + sum(exists(it + ALL_JOBS[q]) for q in same if q < pos)
    if isinstance(i, int):
        return count(i)
    return i * PER_BANK + (count(FIRST_FULL) - FIRST_FULL * PER_BANK)


def place(h):
    return h % HC // 2 * HC + h // HC * 2 + h % 2


def runs(i, phase):
    return exists(i if phase == X else i - 1)


def slot(i, phase, g):
    if isinstance(i, int):
        if phase == X:
            return g if i == 0 else 8 * i - G + g
        return 8 * i + g if i < NB else 8 * i - G + g
    return i * 8 + (g - G if phase == X else g)


def program(nc, x, xT, adj, w):
    ctx = ExitStack()
    with ctx:
        def sb(name, shape, dt=F32):
            return ctx.enter_context(nc.sbuf_tensor(name, shape, dt))

        def bank(name):
            return ctx.enter_context(nc.psum_tensor(name, [P, 512], F32))

        def sem(name):
            return ctx.enter_context(nc.semaphore(name))

        wqkv = [[sb(f"wqkv{l}{p}", [P, C, 3 * D], F32R) for p in "hl"] for l in (0, 1)]
        wo = [[sb(f"wo{l}{p}", [P, C, D], F32R) for p in "hl"] for l in (0, 1)]
        w1 = [sb(f"w1{p}", [P, C, F], F32R) for p in "hl"]
        w2 = [sb(f"w2{p}", [P, FC, D], F32R) for p in "hl"]
        ident = sb("ident", [P, P])
        par = sb("par", [P, 10 * C + FC])
        cols = par[:, 0:8 * C].rearrange("p (n c) -> p n c", c=C)
        lnp = par[:, 8 * C:10 * C].rearrange("p (n c) -> p n c", c=C)
        b1raw = par[:, 10 * C:]
        nbq = sb("nbq", [P, 2, C])
        bk = sb("bk", [P, 2, C])
        pair = sb("pair", [P, 2])
        bkp = sb("bkp", [P, 2, 2, C])
        lgq = sb("lgq", [P, C])
        b1 = sb("b1", [P, FC])
        gamma = sb("gamma", [P, D])
        beta = sb("beta", [P, D])
        bo = [sb(f"bo{l}", [P, D]) for l in (0, 1)]
        b2 = sb("b2", [P, D])
        ones = sb("ones", [P, P])
        power = sb("power", [P, G])
        xy = sb("xy", [P, G, D])
        xTr = sb("xTr", [P, C, T])
        act = [sb(f"act{p}", [P, C, T], F32R) for p in "hl"]
        q = [[sb(f"q{l}{p}", [P, C, T], F32R) for p in "hl"] for l in (0, 1)]
        kp = [[sb(f"kp{l}{p}", [P, C, 2, T], F32R) for p in "hl"] for l in (0, 1)]
        v = [sb(f"v{l}", [P, G, D]) for l in (0, 1)]
        ot = [sb(f"ot{p}", [P, C, T], F32R) for p in "hl"]
        y0 = sb("y0", [P, G, D])
        r1 = sb("r1", [P, G, D])
        x1 = sb("x1", [P, G, D])
        hf = sb("hf", [P, 2, T])
        hh = [sb(f"h{p}", [P, FC, T], F32R) for p in "hl"]
        m0 = sb("m0", [P, G, N])
        a1 = sb("a1", [P, G, N])
        m1 = sb("m1", [P, G, N])
        pm = sb("pm", [P, 2, H, N])
        pt = sb("pt", [P, 2, H, N])
        nmax = sb("nmax", [P, 2, H])
        rsum = sb("rsum", [P, 2, H])
        rinv = sb("rinv", [P, 2, H])
        stats = sb("stats", [P, 3, G, 6])
        mv = sb("mv", [P, 3, G, 2])
        veps = sb("veps", [P, 3, G])
        rstd = sb("rstd", [P, 3, G])

        ps_s = [bank("ps_s0"), bank("ps_s1")]
        ps_t = [bank("ps_t0"), bank("ps_t1")]
        ps_o = bank("ps_o")
        ps_j = [bank(f"ps_j{n}") for n in range(BANKS)]

        qkv_loaded = [sem(f"qkv_loaded{l}") for l in (0, 1)]
        cols_loaded, rows_loaded, wo_loaded, mlp_loaded = (
            sem("cols_loaded"), sem("rows_loaded"), sem("wo_loaded"), sem("mlp_loaded"))
        x_loaded, xT_loaded, adj0_loaded, adj1_loaded = (
            sem("x_loaded"), sem("xT_loaded"), sem("adj0_loaded"), sem("adj1_loaded"))
        out_stored = sem("out_stored")
        ident_done, ones_done, pair_done = sem("ident_done"), sem("ones_done"), sem("pair_done")
        hi_made, hi_copied, lo_made = sem("hi_made"), sem("hi_copied"), sem("lo_made")
        bias_mm, bias_step, bias_act = sem("bias_mm"), sem("bias_step"), sem("bias_act")
        job_full = [sem(f"job_full{n}") for n in range(BANKS)]
        job_free = [sem(f"job_free{n}") for n in range(BANKS)]
        scores_full, masked, exp_done, rinv_done, norm_done = (
            sem("scores_full"), sem("masked"), sem("exp_done"), sem("rinv_done"), sem("norm_done"))
        pt_full, pt_a, pt_b, pv_done, ot_hi, ot_lo = (
            sem("pt_full"), sem("pt_a"), sem("pt_b"), sem("pv_done"), sem("ot_hi"), sem("ot_lo"))
        act_hi = [sem(f"act_hi{n}") for n in range(3)]
        act_lo0 = sem("act_lo0")
        mask0_done, mask1_done, mask1_step = sem("mask0_done"), sem("mask1_done"), sem("mask1_step")
        qk_hi = [sem(f"qk_hi{l}") for l in (0, 1)]
        kp_lo = [sem(f"kp_lo{l}") for l in (0, 1)]
        xb_done = sem("xb_done")
        y0_mul, y0_done, r1_done, x1b_done = (
            sem("y0_mul"), sem("y0_done"), sem("r1_done"), sem("x1b_done"))
        stats_done = [sem(f"stats_done{n}") for n in range(3)]
        aggr_done = [sem(f"aggr_done{n}") for n in range(3)]
        veps_done = [sem(f"veps_done{n}") for n in range(3)]
        rstd_done = [sem(f"rstd_done{n}") for n in range(3)]
        xhat_done = [sem(f"xhat_done{n}") for n in range(3)]
        h_hi, h_lo = sem("h_hi"), sem("h_lo")
        carried = sem("carried")

        def need(eng, s, n):
            if not isinstance(n, int) or n > 0:
                eng.wait_ge(s, n)

        def filled(eng, i, pos):
            eng.wait_ge(job_full[pos % BANKS], uses_before(i, pos) + 1)
            return ps_j[pos % BANKS]

        def taken(eng, i, *places):
            for pos in places:
                eng.wait_ge(job_free[pos % BANKS], uses_before(i, pos) + 1)

        def iterate(eng, body, prepare):
            for i in range(-1, FIRST_FULL):
                prepare.get(i, lambda: None)()
                body(i)
            with eng.Fori(FIRST_FULL, LAST_FULL + 1) as i:
                body(i)
            for i in range(LAST_FULL + 1, NB + 3):
                body(i)

        def act_read(eng, i):
            for off, at, pos in ((-2, i, POS["MLP1"] + FC - 1), (-1, i, POS["QKV1"] + 5), (0, i - 1, POS["QKV0"] + 5)):
                if exists(i + off):
                    filled(eng, at, pos)
                    return

        def flat(t):
            return t[:, :, :].rearrange("p a b -> p (a b)")

        probs = [t[:, :, :, :].rearrange("p a h n -> p (a h n)") for t in (pm, pt)]
        raw_qkv = [t[:, 0:6 * D].rearrange("p (c n) -> p c n", c=C) for t in probs]
        raw_o = [r1[:, 0:2, :], r1[:, 2:4, :]]
        raw_1 = [flat(x1), flat(v[1])]
        raw_2 = [y0[:, 0:2, :], y0[:, 2:4, :]] + [t[:, 6 * D:8 * D].rearrange("p (c n) -> p c n", n=D)
                                                  for t in probs]
        quarters = [slice(k * FC // 4, (k + 1) * FC // 4) for k in range(4)]
        BQ, BK, BV, LG, LB = 0, 2, 4, 6, 7

        block = ctx.enter_context(nc.Block())

        @block.sync
        def _(sp):
            x_b = x.rearrange("(b g) t f -> b t g f", g=G)
            a_b = adj.rearrange("(b g) q k -> b q g k", g=G)
            o_b = w["out"].rearrange("(b g) t f -> b t g f", g=G)
            xT_v = xT.rearrange("(c p) n -> p c n", p=P)

            def row(name):
                return w[name].rearrange("(a n) -> a n", a=1).to_broadcast([P, D])

            def load_qkv(l):
                for n, part in enumerate(("q", "k", "v")):
                    sp.dma_start(raw_qkv[l][:, :, n * D:(n + 1) * D],
                                 w[f"w{part}{l}"].rearrange("(c p) n -> p c n", p=P)).then_inc(qkv_loaded[l], 16)

            def load_first():
                load_qkv(0)
                sp.dma_start(par[:, :], w["columns"]).then_inc(cols_loaded, 16)

            def load_rest():
                for l in (0, 1):
                    sp.dma_start(raw_o[l], w[f"wo{l}"].rearrange("(c p) n -> p c n", p=P)).then_inc(wo_loaded, 16)
                for dst, name in ((bo[0], "bo0"), (gamma, "gamma"), (beta, "beta"), (bo[1], "bo1"), (b2, "b2")):
                    sp.dma_start(dst[:, :], row(name)).then_inc(rows_loaded, 16)
                load_qkv(1)
                for c in range(C):
                    sp.dma_start(raw_1[c], w["w1"][c * P:(c + 1) * P, :]).then_inc(mlp_loaded, 16)
                for raw, part in zip(raw_2, quarters):
                    sp.dma_start(raw, w["w2"].rearrange("(c p) n -> p c n", p=P)[:, part, :]).then_inc(mlp_loaded, 16)

            def body(i):
                if exists(i + 1):
                    need(sp, act_hi[0], 2 * (i + 1))
                    need(sp, act_lo0, 2 * (i + 1))
                    sp.dma_start(xTr[:, :, :], xT_v[:, :, bass.ts(i + 1, T)]).then_inc(xT_loaded, 16)
                if exists(i - 3):
                    taken(sp, i - 1, POS["MLP2"], POS["MLP2"] + 1)
                    sp.dma_start(o_b[bass.ds(i - 3, 1), :, :, :].rearrange("a t g f -> t (a g) f"),
                                 x1[:, :, :]).then_inc(out_stored, 16)
                if exists(i):
                    if exists(i - 1):
                        filled(sp, i, POS["T1"] + C - 1)
                    sp.dma_start(xy[:, :, :], x_b[bass.ds(i, 1), :, :, :].rearrange("a t g f -> t (a g) f")) \
                      .then_inc(x_loaded, 16)
                if exists(i):
                    need(sp, mask1_done, i)
                    sp.dma_start(a1[:, :, :].bitcast(I32),
                                 a_b[bass.ds(i, 1), :, :, :].rearrange("a q g k -> q (a g) k")) \
                      .then_inc(adj1_loaded, 16)
                if exists(i + 1):
                    if exists(i):
                        need(sp, masked, 2 * slot(i, X, G - 1) + 2)
                    sp.dma_start(m0[:, :, :].bitcast(I32),
                                 a_b[bass.ds(i + 1, 1), :, :, :].rearrange("a q g k -> q (a g) k")) \
                      .then_inc(adj0_loaded, 16)

            iterate(sp, body, {-1: load_first, 0: load_rest})
            sp.wait_ge(out_stored, 16 * NB)

        @block.tensor
        def _(pe):
            mm = nc.tensor.matmul

            def first_weights():
                pe.wait_ge(lo_made, 2 * C)

            def shift_products():
                pe.wait_ge(bias_step, 2)
                pe.wait_ge(wo_loaded, 32)
                for c in range(C):
                    last = mm(ps_t[1][:, 0:D], m1[:, c, :], raw_o[0][:, c, :],
                              start=(c == 0), stop=(c == C - 1))
                last.then_inc(bias_mm, 1)
                pe.wait_ge(qkv_loaded[1], 48)
                for n in range(3 * C):
                    for c in range(C):
                        last = mm(ps_t[0][:, n:n + 1], raw_qkv[1][:, c, n * P:(n + 1) * P],
                                  cols[:, LB, c:c + 1], start=(c == 0), stop=(c == C - 1))
                last.then_inc(bias_mm, 1)
                pe.wait_ge(ident_done, 3)
                pe.wait_ge(lo_made, 2 * C + 2)

            def bo1_product():
                pe.wait_ge(bias_step, 5)
                for c in range(C):
                    last = mm(ps_o[:, D:2 * D], m1[:, C + c, :], raw_o[1][:, c, :],
                              start=(c == 0), stop=(c == C - 1))
                last.then_inc(bias_mm, 1)
                pe.wait_ge(lo_made, 4 * C + 2)

            def open_job(i, pos):
                need(pe, job_free[pos % BANKS], uses_before(i, pos))
                return ps_j[pos % BANKS]

            def b1_product(i, ms):
                if isinstance(i, int) and i == 0:
                    if 0 in ms:
                        pe.wait_ge(mlp_loaded, 96)
                        open_job(0, POS["QKV0"])
                    for m in ms:
                        for c in range(C):
                            last = mm(ps_j[POS["QKV0"] % BANKS][:, m:m + 1], raw_1[c][:, m * P:(m + 1) * P],
                                      lnp[:, 1, c:c + 1], start=(c == 0), stop=(c == C - 1))
                    if FC - 1 in ms:
                        last.then_inc(bias_mm, 1)

            def scores(i, phase, g, c):
                if runs(i, phase):
                    l, n = phase, slot(i, phase, g)
                    if g == 0 and c == 0:
                        taken(pe, i - 1 if phase == X else i, *(POS[f"QKV{l}"] + m for m in range(1, 4)))
                        need(pe, kp_lo[l], C * ((i if phase == X else i - 1) + 1))
                    need(pe, masked, 2 * n - C + c + 1)
                    gs = slice(g * N, (g + 1) * N)
                    rows = slice(64 * c, 64 * c + 64)
                    for k in range(C):
                        out = ps_s[c][:, 2 * k * N:2 * (k + 1) * N].rearrange("p (h n) -> p h n", h=2)
                        for t, (a, b) in enumerate(((0, 0), (1, 0), (0, 1))):
                            last = mm(out, q[l][a][rows, k, gs], kp[l][b][rows, k, :, gs],
                                      start=(t == 0), stop=(t == 2))
                    last.then_inc(scores_full, 1)

            def flip(i, phase, g, c):
                if runs(i, phase):
                    n = slot(i, phase, g)
                    need(pe, norm_done, 2 * n + c + 1)
                    need(pe, (pt_a, pt_b)[c], n)
                    for j in range(HC):
                        last = nc.tensor.transpose(ps_t[c][:, j * N:(j + 1) * N],
                                                   pm[:, g % 2, c * HC + j, :], ident[:, :])
                    last.then_inc(pt_full, 1)

            def values(i, phase, g):
                if runs(i, phase):
                    l, n = phase, slot(i, phase, g)
                    if g == 0:
                        taken(pe, i - 1 if phase == X else i, POS[f"QKV{l}"] + 4, POS[f"QKV{l}"] + 5)
                    need(pe, pt_a, n + 1)
                    need(pe, pt_b, n + 1)
                    need(pe, ot_lo, n)
                    for h in range(H):
                        j = h % HC
                        last = mm(ps_o[j * HD:(j + 1) * HD, (h // HC) * N:(h // HC + 1) * N],
                                  v[l][:, g, h * HD:(h + 1) * HD], pt[:, g % 2, place(h), :], start=True, stop=True)
                    last.then_inc(pv_done, 1)

            def split_mm(out, parts, wparts, pick, wpick, chunks):
                terms = [(c, a, b) for c in range(chunks) for a, b in ((0, 0), (0, 1), (1, 0))]
                for n, (c, a, b) in enumerate(terms):
                    last = mm(out, pick(parts[a], c), wpick(wparts[b], c),
                              start=(n == 0), stop=(n == len(terms) - 1))
                return last

            def flip_rows(i, name, c):
                off, src, k = {"T1": (-1, xy, 1), "T2": (-2, r1, 2)}[name]
                if exists(i + off):
                    pos = POS[name] + c
                    need(pe, xhat_done[k], i + off + 1)
                    out = open_job(i, pos)
                    for g in range(G):
                        last = nc.tensor.transpose(out[:, g * N:(g + 1) * N],
                                                   src[:, g, c * P:(c + 1) * P], ident[:, :])
                    last.then_inc(job_full[pos % BANKS], 1)

            def out_proj(i, l, j):
                off = 0 if l == 0 else -2
                if not exists(i + off):
                    return
                pos = POS[f"WO{l}"] + j
                n = slot(i, X, 2 * j + 1) if l == 0 else slot(i - 1, Y, 2 * j + 1)
                need(pe, ot_lo, n + 1)
                out = open_job(i, pos)
                for g in (2 * j, 2 * j + 1):
                    last = split_mm(out[:, (g % 2) * D:(g % 2 + 1) * D], ot, wo[l],
                                    lambda t, c: t[:, c, g * N:(g + 1) * N], lambda t, c: t[:, c, :], C)
                last.then_inc(job_full[pos % BANKS], 1)

            def qkv(i, l, n):
                b = i + (1 if l == 0 else -1)
                if exists(b):
                    pos = POS[f"QKV{l}"] + n
                    if n == 0 and l == 0:
                        need(pe, act_hi[0], C * (b + 1))
                        need(pe, act_lo0, C * (b + 1))
                        if isinstance(i, int) and i == 0:
                            pe.wait_ge(bias_step, 6)
                    elif n == 0:
                        taken(pe, i, POS["T1"], POS["T1"] + 1)
                    out = open_job(i, pos)
                    if n < 4:
                        last = split_mm(out[:, :], wqkv[l], act,
                                        lambda t, c: t[:, c, n * P:(n + 1) * P], lambda t, c: t[:, c, :], C)
                    else:
                        for g in (2 * (n - 4), 2 * (n - 4) + 1):
                            last = split_mm(out[:, (g % 2) * D:(g % 2 + 1) * D], act, wqkv[l],
                                            lambda t, c: t[:, c, g * N:(g + 1) * N],
                                            lambda t, c: t[:, c, 2 * D:3 * D], C)
                    last.then_inc(job_full[pos % BANKS], 1)

            def mlp_up(i, m):
                b = i - 2
                if not exists(b):
                    return
                pos = POS["MLP1"] + m
                if m == 0 and isinstance(i, int):
                    pe.wait_ge(lo_made, 5 * C + 6)
                if m == 0:
                    taken(pe, i, POS["T2"], POS["T2"] + 1)
                out = open_job(i, pos)
                split_mm(out[:, :], w1, act, lambda t, c: t[:, c, m * P:(m + 1) * P],
                         lambda t, c: t[:, c, :], C).then_inc(job_full[pos % BANKS], 1)

            def mlp_down(i, g):
                b = i - 2
                if not exists(b):
                    return
                pos = POS["MLP2"] + g // 2
                out = ps_j[pos % BANKS]
                if g % 2 == 0:
                    need(pe, h_lo, FC * (b + 1))
                    open_job(i, pos)
                last = split_mm(out[:, (g % 2) * D:(g % 2 + 1) * D], hh, w2,
                                lambda t, c: t[:, c, g * N:(g + 1) * N], lambda t, c: t[:, c, :], FC)
                if g % 2 == 1:
                    last.then_inc(job_full[pos % BANKS], 1)

            def body(i):
                flip(i - 1, Y, 2, 0); scores(i, X, 0, 0); flip(i - 1, Y, 2, 1); values(i - 1, Y, 1)
                flip(i - 1, Y, 3, 0); scores(i, X, 0, 1); b1_product(i, (0, 1, 2)); flip_rows(i, "T1", 0)
                scores(i, X, 1, 0); flip_rows(i, "T1", 1); flip(i - 1, Y, 3, 1); values(i - 1, Y, 2)
                out_proj(i, 1, 0); scores(i, X, 1, 1); b1_product(i, (3, 4, 5)); values(i - 1, Y, 3)
                flip(i, X, 0, 0); scores(i, X, 2, 0); flip(i, X, 0, 1); scores(i, X, 2, 1); out_proj(i, 1, 1)
                qkv(i, 1, 0); qkv(i, 1, 1); qkv(i, 1, 2); flip(i, X, 1, 0); scores(i, X, 3, 0); qkv(i, 1, 3)
                flip(i, X, 1, 1); scores(i, X, 3, 1); values(i, X, 0); flip(i, X, 2, 0); flip(i, X, 2, 1)
                qkv(i, 1, 4); qkv(i, 1, 5); values(i, X, 1); b1_product(i, (6, 7)); flip_rows(i, "T2", 0)
                flip_rows(i, "T2", 1); scores(i, Y, 0, 0); scores(i, Y, 0, 1); values(i, X, 2)
                flip(i, X, 3, 0); scores(i, Y, 1, 0); flip(i, X, 3, 1); mlp_up(i, 0); scores(i, Y, 1, 1)
                values(i, X, 3); mlp_up(i, 1); mlp_up(i, 2); mlp_up(i, 3); mlp_up(i, 4); mlp_up(i, 5)
                mlp_up(i, 6); mlp_up(i, 7); out_proj(i, 0, 0); out_proj(i, 0, 1); qkv(i, 0, 0)
                flip(i, Y, 0, 0); qkv(i, 0, 1); flip(i, Y, 0, 1); qkv(i, 0, 2); scores(i, Y, 2, 0)
                qkv(i, 0, 3); scores(i, Y, 2, 1); qkv(i, 0, 4); qkv(i, 0, 5); mlp_down(i, 0); values(i, Y, 0)
                flip(i, Y, 1, 0); scores(i, Y, 3, 0); flip(i, Y, 1, 1); scores(i, Y, 3, 1); mlp_down(i, 1)
                mlp_down(i, 2); mlp_down(i, 3)

            iterate(pe, body, {-1: first_weights, 0: shift_products, 1: bo1_product})

        @block.scalar
        def _(sc):
            def copy_biases(l):
                nc.scalar.activation(nbq[:, l, :], cols[:, BQ + l, :], ACT.Copy, scale=-SCALE).then_inc(bias_act, 1)
                nc.scalar.activation(bk[:, l, :], cols[:, BK + l, :], ACT.Copy).then_inc(bias_act, 1)
                for o in (0, 1):
                    nc.scalar.activation(bkp[:, l, o, :], cols[:, BK + l, :], ACT.Identity, bias=0.0,
                                         scale=pair[:, o:o + 1]).then_inc(bias_act, 1)
                sc.wait_ge(bias_act, 4 * (l + 1))

            def before_first():
                sc.wait_ge(cols_loaded, 16)
                sc.wait_ge(pair_done, 3)
                copy_biases(0)

            def split_wo():
                sc.wait_ge(wo_loaded, 32)
                for l in (0, 1):
                    nc.scalar.activation(wo[l][0][:, :, :], raw_o[l], ACT.Copy).then_inc(hi_copied, 1)

            def layer1_biases():
                sc.wait_ge(bias_step, 4)
                copy_biases(1)

            def split_w2():
                sc.wait_ge(mlp_loaded, 96)
                for raw, part in zip(raw_2, quarters):
                    nc.scalar.activation(w2[0][:, part, :], raw, ACT.Copy).then_inc(hi_copied, 1)

            def split_all():
                split_wo()
                split_w2()

            def b1_ready():
                sc.wait_ge(bias_step, 6)

            def exp(i, phase, g, c):
                if runs(i, phase):
                    need(sc, masked, 2 * slot(i, phase, g) + c + 1)
                    for h in range(c * HC, (c + 1) * HC):
                        last = nc.scalar.activation(pm[:, g % 2, h, :], pm[:, g % 2, h, :], ACT.Exp,
                                                    bias=nmax[:, g % 2, h:h + 1], scale=-1.0,
                                                    accum_out=rsum[:, g % 2, h:h + 1])
                    last.then_inc(exp_done, 1)

            def copy_pt(i, phase, g):
                if runs(i, phase):
                    need(sc, pt_full, 2 * slot(i, phase, g) + 1)
                    nc.scalar.activation(pt[:, g % 2, 0:HC, :], ps_t[0][:, :].rearrange("p (h q) -> p h q", h=HC),
                                         ACT.Copy).then_inc(pt_a, 1)

            def out_hi(i, phase, g):
                if runs(i, phase):
                    need(sc, pv_done, slot(i, phase, g) + 1)
                    nc.scalar.activation(ot[0][:, :, g * N:(g + 1) * N],
                                         ps_o[:, 0:C * N].rearrange("p (c q) -> p c q", c=C),
                                         ACT.Copy).then_inc(ot_hi, 1)

            def qk_hi_out(i, l, n):
                b = i + (1 if l == 0 else -1)
                if exists(b):
                    pos = POS[f"QKV{l}"] + n
                    src = filled(sc, i, pos)
                    c = n % C
                    if n < 2:
                        nc.scalar.activation(q[l][0][:, c, :], src[:, :], ACT.Identity,
                                             bias=nbq[:, l, c:c + 1]).then_inc(qk_hi[l], 1)
                    else:
                        for o in (0, 1):
                            nc.scalar.activation(kp[l][0][:, c, o, :], src[:, :], ACT.Identity,
                                                 bias=bkp[:, l, o, c:c + 1], scale=pair[:, o:o + 1])
                        need(sc, kp_lo[l], C * b)
                        if l == 1 and exists(i):
                            sc.wait_ge(kp_lo[0], C * i + c + 1)
                        if l == 0 and exists(i - 1):
                            sc.wait_ge(kp_lo[1], C * (i - 1) + c + 1)
                        if exists(i - 3 if l == 1 else i - 2):
                            sc.wait_ge(h_lo, FC * (i - 2 if l == 1 else i - 1) - 1 + c)
                        nc.scalar.activation(hf[:, c, :].bitcast(F32R), src[:, :], ACT.Identity,
                                             bias=bk[:, l, c:c + 1]).then_inc(qk_hi[l], 1)

            def hi(i, name, c):
                off, k = {"T1": (-1, 1), "T2": (-2, 2)}[name]
                if exists(i + off):
                    src = filled(sc, i, POS[name] + c)
                    nc.scalar.activation(act[0][:, c, :], src[:, :], ACT.Copy).then_inc(act_hi[k], 1)

            def x_hi(i, c):
                if exists(i + 1):
                    if c == 0:
                        need(sc, xT_loaded, 16 * (i + 2))
                        act_read(sc, i)
                    nc.scalar.activation(act[0][:, c, :], xTr[:, c, :], ACT.Copy).then_inc(act_hi[0], 1)

            def gelu(i, m):
                b = i - 2
                if exists(b):
                    src = filled(sc, i, POS["MLP1"] + m)
                    need(sc, h_lo, FC * b + m - 1)
                    if m < 2 and exists(i - 1):
                        sc.wait_ge(kp_lo[1], C * (i - 1) + m + 1)
                    nc.scalar.activation(hf[:, m % 2, :], src[:, :], ACT.Gelu, bias=b1[:, m:m + 1])\
                      .then_inc(job_free[(POS["MLP1"] + m) % BANKS], 1)

            def body(i):
                copy_pt(i - 1, Y, 2); out_hi(i - 1, Y, 1); exp(i, X, 0, 0); exp(i, X, 0, 1); hi(i, "T1", 0)
                out_hi(i - 1, Y, 2); copy_pt(i - 1, Y, 3); hi(i, "T1", 1); exp(i, X, 1, 0)
                out_hi(i - 1, Y, 3); exp(i, X, 1, 1); copy_pt(i, X, 0); exp(i, X, 2, 0); qk_hi_out(i, 1, 0)
                exp(i, X, 2, 1); qk_hi_out(i, 1, 1); qk_hi_out(i, 1, 2); copy_pt(i, X, 1); qk_hi_out(i, 1, 3)
                out_hi(i, X, 0); exp(i, X, 3, 0); exp(i, X, 3, 1); out_hi(i, X, 1); hi(i, "T2", 0)
                copy_pt(i, X, 2); hi(i, "T2", 1); out_hi(i, X, 2); exp(i, Y, 0, 0); copy_pt(i, X, 3)
                exp(i, Y, 0, 1); gelu(i, 0); gelu(i, 1); gelu(i, 2); out_hi(i, X, 3); gelu(i, 3); gelu(i, 4)
                gelu(i, 5); gelu(i, 6); x_hi(i, 0); x_hi(i, 1); gelu(i, 7); exp(i, Y, 1, 0); exp(i, Y, 1, 1)
                qk_hi_out(i, 0, 0); qk_hi_out(i, 0, 1); qk_hi_out(i, 0, 2); qk_hi_out(i, 0, 3)
                copy_pt(i, Y, 0); exp(i, Y, 2, 0); out_hi(i, Y, 0); exp(i, Y, 2, 1); copy_pt(i, Y, 1)
                exp(i, Y, 3, 0); exp(i, Y, 3, 1)

            iterate(sc, body, {-1: before_first, 0: split_all, 1: layer1_biases, 2: b1_ready})

        @block.vector
        def _(dve):
            tt, ts = nc.vector.tensor_tensor, nc.vector.tensor_scalar

            def split(first, parts):
                own = [p for p in parts if p[4]]
                for h, _, raw, by, _ in own:
                    ts(h, raw, by, None, ALU.mult).then_inc(hi_made, 1)
                dve.wait_ge(hi_made, first[0] + len(own))
                if len(own) < len(parts):
                    dve.wait_ge(hi_copied, first[1] + len(parts) - len(own))
                for h, lo, raw, by, _ in parts:
                    nc.vector.scalar_tensor_tensor(lo, raw, by, h.bitcast(F32), ALU.mult, ALU.subtract)\
                      .then_inc(lo_made, 1)

            def qkv_parts(l, q_scale, scale):
                return [(wqkv[l][0][:, c, n], wqkv[l][1][:, c, n], raw_qkv[l][:, c, n], by(c), True)
                        for c in range(C) for n, by in ((slice(0, D), q_scale), (slice(D, 3 * D), scale))]

            def first_weights():
                dve.wait_ge(qkv_loaded[0], 48)
                split((0, 0), qkv_parts(0, lambda c: -SCALE, lambda c: 1.0))
                dve.wait_ge(cols_loaded, 16)
                ts(lgq[:, :], cols[:, LG, :], -SCALE, None, ALU.mult).then_inc(bias_step, 1)
                dve.wait_ge(ones_done, 1)
                for c in range(C):
                    last = ts(m1[:, c, :], ones[:, :], cols[:, BV, c:c + 1], None, ALU.mult)
                last.then_inc(bias_step, 1)

            def second_weights():
                split((2 * C, 0), [(wo[l][0][:, :, :], wo[l][1][:, :, :], raw_o[l], 1.0, False) for l in (0, 1)])
                dve.wait_ge(rows_loaded, 80)
                dve.wait_ge(bias_mm, 1)
                tt(bo[0][:, :], bo[0][:, :], ps_t[1][:, 0:D], ALU.add).then_inc(bias_step, 1)
                dve.wait_ge(qkv_loaded[1], 48)
                dve.wait_ge(bias_step, 3)
                split((2 * C, 2), qkv_parts(1, lambda c: lgq[:, c:c + 1], lambda c: cols[:, LG, c:c + 1])
                      + [(w2[0][:, part, :], w2[1][:, part, :], raw, 1.0, False)
                         for raw, part in zip(raw_2, quarters)])
                dve.wait_ge(bias_mm, 2)
                for n, to in ((0, BQ + 1), (1, BK + 1), (2, BV + 1)):
                    last = tt(cols[:, to, :], cols[:, to, :], ps_t[0][:, n * C:(n + 1) * C], ALU.add)
                last.then_inc(bias_step, 1)
                dve.wait_ge(bias_step, 4)
                for c in range(C):
                    last = ts(m1[:, C + c, :], ones[:, :], cols[:, BV + 1, c:c + 1], None, ALU.mult)
                last.then_inc(bias_step, 1)

            def add_b1(i):
                if isinstance(i, int) and i == 0:
                    dve.wait_ge(bias_mm, 3)
                    tt(b1[:, :], b1raw, ps_j[POS["QKV0"] % BANKS][:, 0:FC], ALU.add).then_inc(bias_step, 1)

            def split_w1(i, c):
                if isinstance(i, int) and i == 0:
                    dve.wait_ge(mlp_loaded, 96)
                    split((4 * C + c, 6), [(w1[0][:, c, :], w1[1][:, c, :], raw_1[c], lnp[:, 0, c:c + 1], True)])

            def bo1_sum():
                dve.wait_ge(bias_mm, 4)
                tt(bo[1][:, :], bo[1][:, :], ps_o[:, D:2 * D], ALU.add).then_inc(bias_step, 1)

            def mask0(i):
                b = i + 1
                if exists(b):
                    dve.wait_ge(adj0_loaded, 16 * (b + 1))
                    ts(m0[:, :, :], m0[:, :, :].bitcast(I32), 0, BIG, ALU.is_equal, ALU.mult)\
                      .then_inc(mask0_done, 1)

            def mask1(i):
                b = i - 1
                if exists(b):
                    dve.wait_ge(adj1_loaded, 16 * (b + 1))
                    a = a1[:, :, :].bitcast(I32)
                    nc.vector.scalar_tensor_tensor(m1[:, :, :], a, -0.1, a, ALU.mult, ALU.mult)\
                      .then_inc(mask1_step, 1)
                    dve.wait_ge(mask1_step, 2 * b + 1)
                    ts(a1[:, :, :], a, 0, BIG, ALU.is_le, ALU.mult).then_inc(mask1_step, 1)
                    dve.wait_ge(mask1_step, 2 * b + 2)
                    tt(m1[:, :, :], m1[:, :, :], a1[:, :, :], ALU.add).then_inc(mask1_done, 1)

            def mask_scores(i, phase, g, c):
                if runs(i, phase):
                    if g == 0 and c == 0:
                        dve.wait_ge((mask0_done, mask1_done)[phase], (i if phase == X else i - 1) + 1)
                    m = (m0, m1)[phase]
                    dve.wait_ge(scores_full, 2 * slot(i, phase, g) + c + 1)
                    dve.sem_inc(carried, 1)
                    for j in range(HC):
                        h = c * HC + j
                        last = nc.vector.tensor_tensor_reduce(
                            out=pm[:, g % 2, h, :], in0=ps_s[c][:, j * N:(j + 1) * N],
                            in1=m[:, g, :], scale=1.0, scalar=3e38, op0=ALU.add, op1=ALU.min,
                            accum_out=nmax[:, g % 2, h:h + 1])
                    last.then_inc(masked, 1)

            def recip(i, phase, g):
                if runs(i, phase):
                    dve.wait_ge(exp_done, 2 * slot(i, phase, g) + 2)
                    nc.vector.reciprocal(rinv[:, g % 2, :], rsum[:, g % 2, :]).then_inc(rinv_done, 1)

            def copy_pt(i, phase, g):
                if runs(i, phase):
                    dve.wait_ge(pt_full, 2 * slot(i, phase, g) + 2)
                    nc.vector.tensor_copy(pt[:, g % 2, HC:H, :], ps_t[1][:, :].rearrange("p (h q) -> p h q", h=HC))\
                      .then_inc(pt_b, 1)

            def out_lo(i, phase, g):
                if runs(i, phase):
                    dve.wait_ge(ot_hi, slot(i, phase, g) + 1)
                    cols_g = slice(g * N, (g + 1) * N)
                    tt(ot[1][:, :, cols_g], ps_o[:, 0:C * N].rearrange("p (c q) -> p c q", c=C),
                       ot[0][:, :, cols_g].bitcast(F32), ALU.subtract).then_inc(ot_lo, 1)

            def lo(i, name, c):
                off, k = {"T1": (-1, 1), "T2": (-2, 2)}[name]
                b = i + off
                if exists(b):
                    pos = POS[name] + c
                    filled(dve, i, pos)
                    dve.wait_ge(act_hi[k], C * b + c + 1)
                    tt(act[1][:, c, :], ps_j[pos % BANKS][:, :], act[0][:, c, :].bitcast(F32),
                       ALU.subtract).then_inc(job_free[pos % BANKS], 1)

            def x_lo(i, c):
                if exists(i + 1):
                    dve.wait_ge(act_hi[0], C * (i + 1) + c + 1)
                    tt(act[1][:, c, :], xTr[:, c, :], act[0][:, c, :].bitcast(F32), ALU.subtract)\
                      .then_inc(act_lo0, 1)

            def qk_lo(i, l, n):
                b = i + (1 if l == 0 else -1)
                if exists(b):
                    pos, c = POS[f"QKV{l}"] + n, n % C
                    src = filled(dve, i, pos)
                    dve.wait_ge(qk_hi[l], 4 * b + n + 1)
                    if n < 2:
                        nc.vector.scalar_tensor_tensor(q[l][1][:, c, :], src[:, :], nbq[:, l, c:c + 1],
                                                       q[l][0][:, c, :].bitcast(F32), ALU.add, ALU.subtract)\
                          .then_inc(job_free[pos % BANKS], 1)
                    else:
                        nc.vector.scalar_tensor_tensor(hf[:, c, :], src[:, :], bk[:, l, c:c + 1],
                                                       hf[:, c, :], ALU.add, ALU.subtract)\
                          .then_inc(job_free[pos % BANKS], 1)

            def v_out(i, l, j):
                if exists(i + (1 if l == 0 else -1)):
                    pos = POS[f"QKV{l}"] + 4 + j
                    src = filled(dve, i, pos)
                    nc.vector.tensor_copy(v[l][:, 2 * j:2 * j + 2, :],
                                          src[:, :].rearrange("p (g n) -> p g n", g=2))\
                      .then_inc(job_free[pos % BANKS], 1)

            def residual(i, name, j):
                off, out, add = {"WO0": (0, xy, xy), "WO1": (-2, x1, r1), "MLP2": (-2, x1, x1)}[name]
                b = i + off
                if exists(b):
                    ready = {"WO0": xb_done, "WO1": r1_done, "MLP2": x1b_done}[name]
                    dve.wait_ge(ready, b + 1)
                    if name == "WO1":
                        need(dve, out_stored, 16 * b)
                    pos = POS[name] + j
                    src = filled(dve, i, pos)
                    gs = slice(2 * j, 2 * j + 2)
                    tt(out[:, gs, :], src[:, :].rearrange("p (g n) -> p g n", g=2), add[:, gs, :],
                       ALU.add).then_inc(job_free[pos % BANKS], 1)

            NORMS = ((xy, xy, 0), (y0, xy, 0), (x1, r1, -2))

            def norm_stats(i, k):
                src, _, off = NORMS[k]
                b = i + off
                if exists(b):
                    if k == 1:
                        dve.wait_ge(y0_done, b + 1)
                    else:
                        name = ("WO0", None, "WO1")[k]
                        taken(dve, i, POS[name], POS[name] + 1)
                    for g in range(G):
                        last = nc.vector.bn_stats(stats[:, k, g, :], src[:, g, :])
                    last.then_inc(stats_done[k], 1)
                    dve.wait_ge(stats_done[k], b + 1)
                    dve.sem_inc(carried, 1)
                    for g in range(G):
                        last = nc.vector.bn_aggr(mv[:, k, g, :], stats[:, k, g, :])
                    last.then_inc(aggr_done[k], 1)
                    dve.wait_ge(aggr_done[k], b + 1)
                    ts(veps[:, k, :], mv[:, k, :, 1], EPS, None, ALU.add).then_inc(veps_done[k], 1)

            def norm_rows(i, k):
                src, out, off = NORMS[k]
                b = i + off
                if exists(b):
                    dve.wait_ge(rstd_done[k], b + 1)
                    for g in range(G):
                        last = ts(out[:, g, :], src[:, g, :], mv[:, k, g, 0:1], rstd[:, k, g:g + 1],
                                  ALU.subtract, ALU.mult)
                    last.then_inc(xhat_done[k], 1)

            def split_h(i, m):
                b = i - 2
                if exists(b):
                    taken(dve, i, POS["MLP1"] + m)
                    nc.vector.tensor_copy(hh[0][:, m, :], hf[:, m % 2, :]).then_inc(h_hi, 1)
                    dve.wait_ge(h_hi, FC * b + m + 1)
                    tt(hh[1][:, m, :], hf[:, m % 2, :], hh[0][:, m, :].bitcast(F32),
                       ALU.subtract).then_inc(h_lo, 1)

            def body(i):
                recip(i - 1, Y, 2); norm_stats(i - 1, 1); mask0(i - 1); residual(i - 1, "MLP2", 0)
                recip(i - 1, Y, 3); v_out(i - 1, 0, 1); mask1(i); norm_rows(i - 1, 1); mask_scores(i, X, 0, 0)
                residual(i - 1, "MLP2", 1); copy_pt(i - 1, Y, 2); mask_scores(i, X, 0, 1); out_lo(i - 1, Y, 1)
                mask_scores(i, X, 1, 0); copy_pt(i - 1, Y, 3); recip(i, X, 0); out_lo(i - 1, Y, 2)
                lo(i, "T1", 0); mask_scores(i, X, 1, 1); lo(i, "T1", 1); out_lo(i - 1, Y, 3)
                residual(i, "WO1", 0); mask_scores(i, X, 2, 0); residual(i, "WO1", 1); recip(i, X, 1)
                mask_scores(i, X, 2, 1); norm_stats(i, 2); qk_lo(i, 1, 0); copy_pt(i, X, 0); recip(i, X, 2)
                qk_lo(i, 1, 1); mask_scores(i, X, 3, 0); qk_lo(i, 1, 2); copy_pt(i, X, 1); norm_rows(i, 2)
                qk_lo(i, 1, 3); mask_scores(i, X, 3, 1); out_lo(i, X, 0); v_out(i, 1, 0); copy_pt(i, X, 2)
                v_out(i, 1, 1); recip(i, X, 3); out_lo(i, X, 1); split_w1(i, 0); lo(i, "T2", 0)
                mask_scores(i, Y, 0, 0); lo(i, "T2", 1); mask_scores(i, Y, 0, 1); out_lo(i, X, 2)
                copy_pt(i, X, 3); split_w1(i, 1); mask_scores(i, Y, 1, 0); mask_scores(i, Y, 1, 1)
                recip(i, Y, 0); split_h(i, 0); split_h(i, 1); split_h(i, 2); split_h(i, 3); split_h(i, 4)
                split_h(i, 5); out_lo(i, X, 3); split_h(i, 6); x_lo(i, 0); x_lo(i, 1); split_h(i, 7)
                add_b1(i); residual(i, "WO0", 0); residual(i, "WO0", 1); norm_stats(i, 0); qk_lo(i, 0, 0)
                recip(i, Y, 1); qk_lo(i, 0, 1); copy_pt(i, Y, 0); norm_rows(i, 0); qk_lo(i, 0, 2)
                mask_scores(i, Y, 2, 0); qk_lo(i, 0, 3); mask_scores(i, Y, 2, 1); v_out(i, 0, 0)
                out_lo(i, Y, 0); mask_scores(i, Y, 3, 0); copy_pt(i, Y, 1); mask_scores(i, Y, 3, 1)

            iterate(dve, body, {-1: first_weights, 0: second_weights, 1: bo1_sum})

        @block.gpsimd
        def _(pool):
            tt = nc.gpsimd.tensor_tensor
            nc.gpsimd.memset(ones[:, :], 1.0).then_inc(ones_done, 1)
            nc.gpsimd.memset(power[:, :], -0.5)
            nc.gpsimd.memset(pair[:, :], 0.0).then_inc(pair_done, 1)
            pool.wait_ge(pair_done, 1)
            for j in range(HC):
                last = nc.gpsimd.memset(pair[j * HD:(j + 1) * HD, j % 2:j % 2 + 1], 1.0)
            last.then_inc(pair_done, 2)
            pool.wait_ge(pair_done, 3)
            nc.gpsimd.memset(ident[:, :], 0.0).then_inc(ident_done, 1)
            pool.wait_ge(ident_done, 1)
            nc.gpsimd.affine_select(out=ident[:, :], in_=ident[:, :], compare_op=ALU.not_equal, fill=1.0,
                                    base=0, pattern=[[-1, P]], channel_multiplier=1).then_inc(ident_done, 2)

            def rows_ready():
                pool.wait_ge(rows_loaded, 80)
                pool.wait_ge(bias_step, 3)

            def bo1_ready():
                pool.wait_ge(bias_step, 7)

            def over_rows(t):
                return t[:, :].rearrange("p (a n) -> p a n", a=1).to_broadcast([P, G, D])

            def normalise(i, phase, g, c):
                if runs(i, phase):
                    pool.wait_ge(rinv_done, slot(i, phase, g) + 1)
                    hs = slice(c * HC, (c + 1) * HC)
                    tt(pm[:, g % 2, hs, :], pm[:, g % 2, hs, :],
                       rinv[:, g % 2, hs].rearrange("p (h a) -> p h a", a=1).to_broadcast([P, HC, N]),
                       ALU.mult).then_inc(norm_done, 1)

            def pad_k(i, l, n):
                b, c = i + (1 if l == 0 else -1), n % C
                if exists(b):
                    taken(pool, i, POS[f"QKV{l}"] + n)
                    tt(kp[l][1][:, c, :, :], hf[:, c:c + 1, :].to_broadcast([P, 2, T]),
                       pair[:, :].rearrange("p (o a) -> p o a", a=1).to_broadcast([P, 2, T]),
                       ALU.mult).then_inc(kp_lo[l], 1)

            def root(i, k):
                b = i + (0, 0, -2)[k]
                if exists(b):
                    pool.wait_ge(veps_done[k], b + 1)
                    tt(rstd[:, k, :], veps[:, k, :], power[:, :], ALU.pow).then_inc(rstd_done[k], 1)

            def add_bo1(i):
                if exists(i - 1):
                    if exists(i - 2):
                        filled(pool, i, POS["T2"] + C - 1)
                    pool.wait_ge(y0_done, i)
                    tt(r1[:, :, :], y0[:, :, :], over_rows(bo[1]), ALU.add).then_inc(r1_done, 1)

            def add_b2(i):
                if exists(i - 2):
                    pool.wait_ge(xhat_done[2], i - 1)
                    tt(x1[:, :, :], x1[:, :, :], over_rows(b2), ALU.add).then_inc(x1b_done, 1)

            def add_bo0(i):
                if exists(i):
                    pool.wait_ge(x_loaded, 16 * (i + 1))
                    tt(xy[:, :, :], xy[:, :, :], over_rows(bo[0]), ALU.add).then_inc(xb_done, 1)

            def scale_y0(i):
                if exists(i):
                    pool.wait_ge(xhat_done[0], i + 1)
                    tt(y0[:, :, :], xy[:, :, :], over_rows(gamma), ALU.mult).then_inc(y0_mul, 1)

            def shift_y0(i):
                if exists(i):
                    pool.wait_ge(y0_mul, i + 1)
                    tt(y0[:, :, :], y0[:, :, :], over_rows(beta), ALU.add).then_inc(y0_done, 1)

            def body(i):
                normalise(i - 1, Y, 2, 0); root(i - 1, 1); normalise(i - 1, Y, 2, 1)
                normalise(i - 1, Y, 3, 0); normalise(i - 1, Y, 3, 1); normalise(i, X, 0, 0)
                normalise(i, X, 0, 1); normalise(i, X, 1, 0); normalise(i, X, 1, 1); root(i, 2)
                normalise(i, X, 2, 0); normalise(i, X, 2, 1); pad_k(i, 1, 2); pad_k(i, 1, 3)
                normalise(i, X, 3, 0); normalise(i, X, 3, 1); add_bo0(i); normalise(i, Y, 0, 0); add_bo1(i)
                normalise(i, Y, 0, 1); add_b2(i); root(i, 0); normalise(i, Y, 1, 0); normalise(i, Y, 1, 1)
                scale_y0(i); shift_y0(i); pad_k(i, 0, 2); pad_k(i, 0, 3)

            iterate(pool, body, {0: rows_ready, 1: bo1_ready})


WEIGHTS = {
    "wq0": "L0_gnn_Wq", "bq0": "L0_gnn_bq", "wk0": "L0_gnn_Wk", "bk0": "L0_gnn_bk",
    "wv0": "L0_gnn_Wv", "bv0": "L0_gnn_bv", "wo0": "L0_gnn_Wo", "bo0": "L0_gnn_bo",
    "gamma": "L0_gnn_gamma", "beta": "L0_gnn_beta",
    "ln1_g": "L1_gnn_ln1_g", "ln1_b": "L1_gnn_ln1_b", "ln2_g": "L1_gnn_ln2_g", "ln2_b": "L1_gnn_ln2_b",
    "wq1": "L1_gnn_wq", "bq1": "L1_gnn_bq", "wk1": "L1_gnn_wk", "bk1": "L1_gnn_bk",
    "wv1": "L1_gnn_wv", "bv1": "L1_gnn_bv", "wo1": "L1_gnn_wo", "bo1": "L1_gnn_bo",
    "w1": "L1_gnn_w1", "b1": "L1_gnn_b1", "w2": "L1_gnn_w2", "b2": "L1_gnn_b2",
}

COLUMNS = ("bq0", "bq1", "bk0", "bk1", "bv0", "bv1", "ln1_g", "ln1_b", "ln2_g", "ln2_b", "b1")


def kernel(**inputs):
    import concourse.bacc as _bacc
    from concourse.bass_utils import run_bass_kernel_spmd as _run

    nc = _bacc.Bacc("TRN2", target_bir_lowering=False, num_devices=1, dynamic_dma_scratch_size=1024)
    x = np.ascontiguousarray(inputs["x"])
    arrays = {"x": x, "xT": np.ascontiguousarray(x.reshape(B * N, D).T),
              "adj": np.ascontiguousarray(inputs["adj"])}
    for short, name in WEIGHTS.items():
        if short not in COLUMNS:
            arrays[short] = np.ascontiguousarray(inputs[name])
    arrays["columns"] = np.ascontiguousarray(
        np.concatenate([inputs[WEIGHTS[short]].reshape(-1, P).T for short in COLUMNS], axis=1))
    arrays = {f"in_{k}": a for k, a in arrays.items()}
    aps = {k[3:]: nc.dram_tensor(k, a.shape, mybir.dt.from_np(a.dtype), kind="ExternalInput").ap()
           for k, a in arrays.items()}
    aps["out"] = nc.dram_tensor("out", (B, N, D), F32, kind="ExternalOutput").ap()
    program(nc, aps.pop("x"), aps.pop("xT"), aps.pop("adj"), aps)
    r = _run(nc, [arrays], core_ids=[0])
    return r.results[0]["out"]
```
